# Optimizing a Trainium2 kernel written in Bass

```python
import numpy as np
import jax
import jax.numpy as jnp

def _softmax(x, axis=-1):
    return jax.nn.softmax(x, axis=axis)

def _gelu(x):
    return jax.nn.gelu(x, approximate=True)

def _silu(x):
    return jax.nn.silu(x)

def _sigmoid(x):
    return jax.nn.sigmoid(x)

def _layernorm(x, axis=-1, eps=1e-05):
    m = jnp.mean(x, axis=axis, keepdims=True)
    v = jnp.var(x, axis=axis, keepdims=True)
    return (x - m) / jnp.sqrt(v + eps)

def _scatter_add(tgt, idx, src, axis=0):
    return tgt.at[idx].add(src)

def _segment_sum(src, seg, n):
    return jax.ops.segment_sum(src, seg, n)
kernel_name = 'mk_gnn_preln_d1_gnn_r8_93fdd7'

def setup_inputs(seed: int=0):
    np.random.seed(seed)
    _w = jnp.asarray

    def _rec_inputs():
        import jax
        import jax.numpy as jnp
        _gk = jax.random.key(seed)
        x = -0.000202 + 1 * jax.random.normal(jax.random.fold_in(_gk, 1), (6250, 128), jnp.float32)
        _s = jax.random.randint(jax.random.fold_in(_gk, 2), (100000,), 0, 6250, jnp.int32)
        _d = jax.random.randint(jax.random.fold_in(_gk, 3), (100000,), 0, 6250, jnp.int32)
        _loop = jnp.arange(6250, dtype=jnp.int32)
        src = jnp.concatenate([_s, _d, _loop])
        dst = jnp.concatenate([_d, _s, _loop])
        _o = jnp.argsort(dst, stable=True)
        src = src[_o]
        dst = dst[_o]
        edge_type_3 = jax.random.randint(jax.random.fold_in(_gk, 12), (206250,), 0, 3, jnp.int32)
        node_type_3 = jax.random.randint(jax.random.fold_in(_gk, 13), (6250,), 0, 3, jnp.int32)
        return (x, src, dst, edge_type_3, node_type_3)
    x, src, dst, edge_type_3, node_type_3 = _rec_inputs()

    def _L0_gnn_setup():
        import jax, jax.numpy as jnp
        import numpy as np
        N_NODES = 6250
        N_EDGES = 100000
        D = 128
        T = 3
        NODE_IN = D + T * D
        key = jax.random.key(seed)
        ks = jax.random.split(key, 8)
        scale = 0.05
        return {'node_feature': jax.random.normal(ks[0], (N_NODES, D), jnp.float32), 'W_e': jax.random.normal(ks[1], (T, D, D), jnp.float32) * scale, 'b_e': jnp.zeros((T, D), jnp.float32), 'W_n': jax.random.normal(ks[2], (T, D, NODE_IN), jnp.float32) * scale, 'b_n': jnp.zeros((T, D), jnp.float32), 'edge_src': jax.random.randint(ks[3], (N_EDGES,), 0, N_NODES, jnp.int32), 'edge_dst': jax.random.randint(ks[4], (N_EDGES,), 0, N_NODES, jnp.int32), 'edge_type': jax.random.randint(ks[5], (N_EDGES,), 0, T, jnp.int32), 'node_type': jax.random.randint(ks[6], (N_NODES,), 0, T, jnp.int32)}
    _L0_gnn_all = _L0_gnn_setup()
    _L0_gnn_in = {k: v for k, v in _L0_gnn_all.items() if k in ('W_e', 'b_e', 'W_n', 'b_n')}
    del _L0_gnn_all
    return {'x': x, 'src': src, 'dst': dst, 'edge_type_3': edge_type_3, 'node_type_3': node_type_3, 'L0_gnn_W_e': _L0_gnn_in['W_e'], 'L0_gnn_b_e': _L0_gnn_in['b_e'], 'L0_gnn_W_n': _L0_gnn_in['W_n'], 'L0_gnn_b_n': _L0_gnn_in['b_n']}

def reference(x, src, dst, edge_type_3, node_type_3, L0_gnn_W_e, L0_gnn_b_e, L0_gnn_W_n, L0_gnn_b_n):
    import jax
    import jax.numpy as jnp

    def _L0_gnn_ref(node_feature, W_e, b_e, W_n, b_n, edge_src, edge_dst, edge_type, node_type):
        import jax, jax.numpy as jnp
        import numpy as np
        N_NODES = 6250
        N_EDGES = 100000
        D = 128
        T = 3
        NODE_IN = D + T * D
        N, Din = node_feature.shape
        n_types = W_e.shape[0]
        out_dim = W_e.shape[1]
        src = node_feature[edge_src]
        parts = [jax.nn.relu(node_feature)]
        for t in range(n_types):
            msg = jax.nn.relu(src @ W_e[t].T + b_e[t])
            msg = jnp.where((edge_type == t)[:, None], msg, jnp.zeros((), msg.dtype))
            parts.append(jax.ops.segment_sum(msg, edge_dst, num_segments=N))
        agg = jnp.concatenate(parts, axis=1)
        updated = jnp.zeros((N, out_dim), node_feature.dtype)
        for t in range(n_types):
            o = agg @ W_n[t].T + b_n[t]
            updated = jnp.where((node_type == t)[:, None], o, updated)
        return updated + node_feature
    h = jnp.maximum(_layernorm(x, axis=-1), 0.0)
    x = x + _L0_gnn_ref(h, L0_gnn_W_e, L0_gnn_b_e, L0_gnn_W_n, L0_gnn_b_n, src, dst, edge_type_3, node_type_3)
    return x

_drawn_inputs = setup_inputs


def setup_inputs(seed=0):
    import zlib

    import numpy as np

    out = dict(_drawn_inputs(seed))
    spreads = {'L0_gnn_b_e': (0.0, 0.1), 'L0_gnn_b_n': (0.0, 0.1)}
    factors = {}
    for name, (base, spread) in spreads.items():
        noise = np.random.default_rng([zlib.crc32(name.encode()), seed]).standard_normal(out[name].shape)
        drawn = base * np.exp(spread * noise) if base else spread * noise
        out[name] = jnp.asarray(drawn.astype(out[name].dtype))
    for name, factor in factors.items():
        out[name] = (out[name] * factor).astype(out[name].dtype)
    return out
```

```python
import concourse.bass as bass
from concourse import mybir
from contextlib import ExitStack

F32 = mybir.dt.float32
I32 = mybir.dt.int32
ALU = mybir.AluOpType
ACT = mybir.ActivationFunctionType
AX_X = mybir.AxisListType.X

P = 128
T = 3
EPS = 1e-5
TPG = 4
GE = TPG * P
SLOTS = 8
WIN = 32
WC = WIN * T
PAD_TYPE = -100000
UN = 4


def build(nc, x, src, dst, etype, ntype, w_e, b_e, w_n, b_n, out):
    N, D = x.shape
    E = src.shape[0]
    NB = -(-N // P)
    NF = N // P
    NR = N - NF * P
    G = -(-E // GE)
    GF = E // GE
    ER = E - GF * GE
    GB = -(-G // P)
    TD = T * D
    AW = max(N + WIN, NB * P) * T
    NP = D // P + T
    assert D == P and NR and ER and NB % UN == 1 and GF < GB * P

    table = nc.dram_tensor("message_table", [N, TD], F32, kind="Internal").ap()
    table_rows = table.rearrange("n (t d) -> (n t) d", t=T)

    with ExitStack() as ctx:
        def sb(name, shape, dt=F32):
            return ctx.enter_context(nc.sbuf_tensor(name, shape, dt))

        def sem(name):
            return ctx.enter_context(nc.semaphore(name))

        acc = sb("acc", [P, AW])
        xb = sb("xb", [P, NB * D])
        hT = sb("hT", [P, NB * P])
        rows = sb("rows", [P, SLOTS, TPG, D])
        onehot = sb("onehot", [P, 4, TPG, WC])
        onehot_x = sb("onehot_x", [P, TPG, WC])
        iota_w = sb("iota_w", [P, WC])
        iota_p = sb("iota_p", [P, P])
        iota_c = sb("iota_c", [P, 1])
        ident = sb("ident", [P, P])
        EW = GB * GE
        e_src, e_dst, e_typ = (acc[:, k * EW:(k + 1) * EW].rearrange("p (b j) -> p b j", b=GB).bitcast(I32)
                               for k in range(3))
        e_idx, e_key = (acc[:, k * EW:(k + 1) * EW].rearrange("p (b j) -> p b j", b=GB) for k in range(2))
        lo = sb("lo", [P, GB])
        hi = sb("hi", [P, GB])
        lo3 = sb("lo3", [P, GB])
        span = sb("span", [P, GB])
        idx = sb("idx", [P, GB * P, TPG], I32)
        key = sb("key", [P, GB * P, TPG])
        idx_now = sb("idx_now", [P, SLOTS, TPG], I32)
        key_x = sb("key_x", [P, 2, TPG])
        ctrl = sb("ctrl", [1, 2, GB * P], I32)
        span_i = sb("span_i", [1, GB * P], I32)
        we_raw = sb("we_raw", [P, T, D])
        wn_raw = sb("wn_raw", [P, T, NP * D])
        weT = sb("weT", [P, TD])
        wnT = sb("wnT", [P, NP, TD])
        be = sb("be", [P, TD])
        bn = sb("bn", [P, TD])
        nt_raw = sb("nt_raw", [P, P], I32)
        nt_f = sb("nt_f", [P, P])
        ntT = sb("ntT", [P, NB])
        mask = sb("mask", [P, T, NB])
        stats = sb("stats", [P, 2, 6])
        mv = sb("mv", [P, NB, 2])
        std = sb("std", [P, NB])
        rstd = sb("rstd", [P, NB])
        nbias = sb("nbias", [P, NB])
        eps = sb("eps", [P, 1])
        h = sb("h", [P, 4, D])
        hTs = sb("hTs", [P, 4, P])
        msum = sb("msum", [P, 2, TD])
        msg = sb("msg", [P, 4, TD])
        fin = msg
        stage = sb("stage", [P, 2, T, P])

        psT = [ctx.enter_context(nc.psum_tensor(f"psT{i}", [P, 512], F32)) for i in range(2)]
        psM = [ctx.enter_context(nc.psum_tensor(f"psM{i}", [P, 512], F32)) for i in range(2)]
        psE = [ctx.enter_context(nc.psum_tensor(f"psE{i}", [P, 512], F32)) for i in range(4)]

        edges_in = sem("edges_in")
        x_in = [sem(f"x_in{i}") for i in range(2)]
        w_in = sem("w_in")
        small_in = sem("small_in")
        consts = sem("consts")
        ident_ok = sem("ident_ok")
        types_ok = sem("types_ok")
        pads = sem("pads")
        xpad = sem("xpad")
        acc_zero = sem("acc_zero")
        dv = sem("dv")
        w_t = sem("w_t")
        w_c = sem("w_c")
        stat = sem("stat")
        agg2 = sem("agg2")
        var_ok = sem("var_ok")
        std_ok = sem("std_ok")
        norm_ok = sem("norm_ok")
        prep_t = sem("prep_t")
        idx_c = sem("idx_c")
        key_c = sem("key_c")
        key_ok = sem("key_ok")
        lo_ok = sem("lo_ok")
        ctrl_ok = sem("ctrl_ok")
        h_ok = sem("h_ok")
        h_t = sem("h_t")
        hT_ok = sem("hT_ok")
        hT_all = sem("hT_all")
        tab_mm = sem("tab_mm")
        tab_sum = sem("tab_sum")
        tab_msg = sem("tab_msg")
        xh_ok = sem("xh_ok")
        tab_out = [sem(f"tab_out{i}") for i in range(4)]
        own_st = sem("own_st")
        own_mm = sem("own_mm")
        own_rd = sem("own_rd")
        own_add = sem("own_add")
        idx_st = sem("idx_st")
        landed = [sem(f"landed{i}") for i in range(SLOTS)]
        hot_ok = sem("hot_ok")
        grp_mm = sem("grp_mm")
        grp_add = sem("grp_add")
        xkey = sem("xkey")
        xhot_ok = sem("xhot_ok")
        x_mm = sem("x_mm")
        x_add = sem("x_add")
        fin_st = sem("fin_st")
        fin_mm = sem("fin_mm")
        fin_acc = sem("fin_acc")
        fin_ok = sem("fin_ok")
        fin_out = [sem(f"fin_out{i}") for i in range(4)]

        def blk(i):
            return bass.ds(i * D, D)

        def steps(eng, first, last, unroll, step):
            loops = (last - first) // unroll
            if loops > 1:
                with eng.Fori(0, loops) as r:
                    for s in range(unroll):
                        step(r * unroll + (first + s), (first + s) % unroll)
                done = first + loops * unroll
            else:
                done = first
            for i in range(done, last):
                step(i, i % unroll)

        XH = (NF // 2) * P
        block = ctx.enter_context(nc.Block())

        @block.sync
        def _(sp):
            def rows_of(a, b, e0, n):
                return a[0:n, b, :], e0[b * P * GE:(b * P + n) * GE].rearrange("(r j) -> r j", j=GE)
            sp.wait_ge(xpad, 1)
            sp.dma_start(xb[:, 0:XH], x[0:XH, :].rearrange("(b p) d -> p b d", p=P)).then_inc(x_in[0], 16)
            sp.dma_start(xb[:, XH:NF * D], x[XH:NF * P, :].rearrange("(b p) d -> p b d", p=P)).then_inc(x_in[1], 16)
            sp.dma_start(xb[0:NR, NF * D:NB * D], x[NF * P:N, :]).then_inc(x_in[1], 16)
            sp.wait_ge(pads, 3)
            for a, e0 in ((e_dst, dst), (e_typ, etype), (e_src, src)):
                for b in range(GB):
                    n = min(P, GF - b * P)
                    o, i = rows_of(a, b, e0, n)
                    sp.dma_start(o, i).then_inc(edges_in, 16)
                r, b = GF % P, GF // P
                sp.dma_start(a[r:r + 1, b, 0:ER], e0[GF * GE:E].rearrange("(r j) -> r j", r=1)).then_inc(edges_in, 16)
            sp.dma_start(e_dst[GF % P:GF % P + 1, GF // P, ER:GE],
                         dst[E - (GE - ER):E].rearrange("(r j) -> r j", r=1)).then_inc(edges_in, 16)

            def store(i, s):
                sp.wait_ge(tab_msg, i + 1)
                sp.dma_start(table[bass.ds(i * P, P), :], msg[:, s, :]).then_inc(tab_out[s], 16)
            steps(sp, 0, NF, UN, store)
            sp.wait_ge(tab_msg, NB)
            sp.dma_start(table[NF * P:N, :], msg[0:NR, NF % UN, :]).then_inc(tab_out[NF % UN], 16)

            def store_out(i, s):
                sp.wait_ge(fin_ok, i + 1)
                sp.dma_start(out[bass.ds(i * P, P), :], fin[:, s, 0:D]).then_inc(fin_out[s], 16)
            steps(sp, 0, NF, UN, store_out)
            sp.wait_ge(fin_ok, NB)
            sp.dma_start(out[NF * P:N, :], fin[0:NR, NF % UN, 0:D]).then_inc(fin_out[NF % UN], 16)
            for s in range(4):
                sp.wait_ge(fin_out[s], 16 * len(range(s, NB, 4)))

        @block.gpsimd
        def _(pool):
            pool.memset(xb[:, NF * D:NB * D], 0.0).then_inc(xpad, 1)
            pool.memset(e_dst[:, GB - 1, :], 0).then_inc(pads, 1)
            pool.memset(e_typ[:, GB - 1, :], PAD_TYPE).then_inc(pads, 1)
            pool.memset(e_src[:, GB - 1, :], 0).then_inc(pads, 1)
            pool.iota(iota_p[:, :], [[1, P]], base=0, channel_multiplier=0,
                      allow_small_or_imprecise_dtypes=True).then_inc(consts, 1)
            pool.iota(iota_c[:, :], [[0, 1]], base=0, channel_multiplier=1,
                      allow_small_or_imprecise_dtypes=True).then_inc(consts, 1)
            pool.iota(iota_w[:, :], [[1, WC]], base=0, channel_multiplier=0,
                      allow_small_or_imprecise_dtypes=True).then_inc(consts, 1)
            pool.memset(acc[:, 3 * EW:AW], 0.0).then_inc(acc_zero, 1)
            for s in range(4):
                pool.wait_ge(tab_out[s], 16 * len(range(s, NB, 4)))
            due = pool.alloc_register("due")
            pool.reg_mov(due, 1)

            def gather(g, s):
                if isinstance(g, int):
                    pool.wait_ge(idx_st, g + 1)
                else:
                    pool.wait_ge(idx_st, pool.snap(due, min_val=1))
                    pool.reg_add(due, due, 1)
                for u in range(TPG):
                    pool.indirect_dma_start(
                        out=rows[:, s, u, :], out_offset=None, in_=table_rows,
                        in_offset=bass.IndirectOffsetOnAxis(ap=idx_now[:, s, u:u + 1], axis=0),
                    ).then_inc(landed[s], 16)
            steps(pool, 0, G, SLOTS, gather)

        @block.tensor
        def _(pe):
            n = [0]

            def t_in(bank):
                if n[0] >= 2:
                    pe.wait_ge(w_c, n[0] - 1)
                n[0] += 1

            pe.wait_ge(ident_ok, 1)
            pe.wait_ge(w_in, 32)
            for t in range(T):
                t_in(t)
                pe.transpose(psT[(n[0] - 1) % 2][:, 0:P], we_raw[:, t, :], ident[:, :]).then_inc(w_t, 1)
            for t in range(T):
                for p in range(NP):
                    t_in(t)
                    pe.transpose(psT[(n[0] - 1) % 2][:, 0:P], wn_raw[:, t, p * D:(p + 1) * D],
                                 ident[:, :]).then_inc(w_t, 1)
            t_in(0)
            pe.wait_ge(types_ok, 1)
            pe.transpose(psT[(n[0] - 1) % 2][:, 0:P], nt_f[:, :], ident[:, :]).then_inc(w_t, 1)

            def tr(i, s):
                pe.wait_ge(h_ok, i + 1)
                if not isinstance(i, int) or i >= 2:
                    pe.wait_ge(hT_ok, i - 1)
                else:
                    pe.wait_ge(w_c, n[0])
                pe.transpose(psT[s % 2][:, 0:P], h[:, s, :], ident[:, :]).then_inc(h_t, 1)

            def mm(i, s):
                pe.wait_ge(hT_ok, i + 1)
                if not isinstance(i, int) or i >= 2:
                    pe.wait_ge(tab_sum, i - 1)
                pe.matmul(psM[s % 2][:, 0:TD], hTs[:, s, :], weT[:, :], start=True, stop=True).then_inc(tab_mm, 1)

            def both(i, s):
                tr(i + 1, (s + 1) % UN)
                mm(i, s)
            tr(0, 0)
            both(0, 0)
            both(1, 1)
            steps(pe, 2, NB - 1, UN, lambda i, s: both(i, s))
            mm(NB - 1, (NB - 1) % UN)

            k = 0
            pe.wait_ge(key_ok, 1)
            for a in (e_idx, e_key):
                for b in range(GB):
                    if k >= GB + 2:
                        pe.wait_ge(key_c, k - GB - 1)
                    elif k >= 2:
                        pe.wait_ge(idx_c, k - 1)
                    for u in range(TPG):
                        m = pe.transpose(psE[k % 2][:, u * P:(u + 1) * P], a[:, b, u * P:(u + 1) * P], ident[:, :])
                    m.then_inc(prep_t, 1)
                    k += 1
            for a, q in ((lo3, 2), (span, 3)):
                for b in range(GB):
                    m = pe.matmul(psE[q][0:1, b * P:(b + 1) * P], a[:, b:b + 1], ident[:, :], start=True, stop=True)
                m.then_inc(prep_t, 1)

            def own(i, s):
                pe.wait_ge(own_st, i + 1)
                if not isinstance(i, int) or i >= 2:
                    pe.wait_ge(own_rd, i - 1)
                pe.matmul(psM[s % 2][:, 0:TD], stage[:, s % 2, 0, :], wnT[:, 0, :],
                          start=True, stop=True).then_inc(own_mm, 1)
            pe.wait_ge(tab_sum, NB)
            own(0, 0)
            own(1, 1)
            steps(pe, 2, NB, UN, own)

            pe.wait_ge(key_c, GB)
            pe.wait_ge(ctrl_ok, 2)
            passes = pe.alloc_register("passes")
            pe.reg_mov(passes, 0)

            def group(g, s):
                more = pe.value_load(ctrl[0:1, 1, bass.ds(g, 1)], min_val=0, max_val=N // WIN)
                pe.wait_ge(landed[s], (g - s) * (16 * TPG // SLOTS) + 16 * TPG)
                with pe.If(more > 0):
                    with pe.Fori(0, more) as _k:
                        pe.reg_add(passes, passes, 1)
                        c = pe.snap(passes, min_val=1)
                        pe.wait_ge(xhot_ok, c)
                        for u in range(TPG):
                            m = pe.matmul(psT[0][:, 0:WC], rows[:, s, u, :], onehot_x[:, u, :],
                                          start=(u == 0), stop=(u == TPG - 1))
                        m.then_inc(x_mm, 1)
                pe.wait_ge(hot_ok, g + 1)
                if not isinstance(g, int) or g >= 4:
                    pe.wait_ge(grp_add, g - 3)
                for u in range(TPG):
                    m = pe.matmul(psE[s % 4][:, 0:WC], rows[:, s, u, :], onehot[:, s % 4, u, :],
                                  start=(u == 0), stop=(u == TPG - 1))
                m.then_inc(grp_mm, 1)
            for g in range(SLOTS):
                group(g, g)
            steps(pe, SLOTS, G, SLOTS, group)

            def finish(i, s):
                pe.wait_ge(fin_st, i + 1)
                if not isinstance(i, int) or i >= 2:
                    pe.wait_ge(fin_acc, i - 1)
                for t in range(T):
                    m = pe.matmul(psM[s % 2][:, 0:TD], stage[:, s % 2, t, :], wnT[:, 1 + t, :],
                                  start=(t == 0), stop=(t == T - 1))
                m.then_inc(fin_mm, 1)
            pe.wait_ge(own_rd, NB)
            finish(0, 0)
            finish(1, 1)
            steps(pe, 2, NB, UN, finish)

        @block.scalar
        def _(act):
            act.dma_start(we_raw[:, :, :], w_e.rearrange("t o i -> o t i")).then_inc(w_in, 16)
            act.dma_start(wn_raw[:, :, :], w_n.rearrange("t o i -> o t i")).then_inc(w_in, 16)
            act.wait_ge(dv, 2)
            act.dma_start(nt_raw[0:NF, :], ntype[0:NF * P].rearrange("(b p) -> b p", p=P)).then_inc(small_in, 16)
            act.dma_start(nt_raw[NF:NB, 0:NR], ntype[NF * P:N].rearrange("(b p) -> b p", b=1)).then_inc(small_in, 16)
            act.dma_start(be[:, :], b_e.rearrange("(a t) o -> a (t o)", a=1).to_broadcast([P, TD])).then_inc(small_in, 16)
            act.dma_start(bn[:, :], b_n.rearrange("(a t) o -> a (t o)", a=1).to_broadcast([P, TD])).then_inc(small_in, 16)
            n = 0
            for t in range(T):
                n += 1
                act.wait_ge(w_t, n)
                act.copy(weT[:, t * D:(t + 1) * D], psT[(n - 1) % 2][:, 0:P]).then_inc(w_c, 1)
            for t in range(T):
                for p in range(NP):
                    n += 1
                    act.wait_ge(w_t, n)
                    act.copy(wnT[:, p, t * D:(t + 1) * D], psT[(n - 1) % 2][:, 0:P]).then_inc(w_c, 1)
            n += 1
            act.wait_ge(w_t, n)
            act.copy(ntT[:, :], psT[(n - 1) % 2][:, 0:NB]).then_inc(w_c, 1)
            act.wait_ge(var_ok, 1)
            act.activation(std[:, :], mv[:, :, 1], ACT.Sqrt, bias=eps[:, 0:1]).then_inc(std_ok, 1)

            def norm(i, s):
                if not isinstance(i, int) or i >= 4:
                    act.wait_ge(h_t, i - 3)
                    act.wait_ge(xh_ok, i - 3)
                act.activation(h[:, s, :], xb[:, blk(i)], ACT.Relu, scale=rstd[:, bass.ds(i, 1)],
                               bias=nbias[:, bass.ds(i, 1)]).then_inc(h_ok, 1)

            def copy_t(i, s):
                act.wait_ge(h_t, i + 1)
                if not isinstance(i, int) or i >= 4:
                    act.wait_ge(tab_mm, i - 3)
                act.copy(hTs[:, s, :], psT[s % 2][:, 0:P]).then_inc(hT_ok, 1)

            def relu(i, s):
                act.wait_ge(tab_sum, i + 1)
                if not isinstance(i, int) or i >= 4:
                    act.wait_ge(tab_out[s], (i - s) * (16 // UN))
                act.activation(msg[:, s, :], msum[:, s % 2, :], ACT.Relu).then_inc(tab_msg, 1)

            def step(i, s):
                if not isinstance(i, int) or i + 1 < NB:
                    norm(i + 1, (s + 1) % UN)
                copy_t(i, s)
                if not isinstance(i, int) or i >= 1:
                    relu(i - 1, (s - 1) % UN)
            act.wait_ge(norm_ok, 1)
            norm(0, 0)
            for i in range(5):
                step(i, i % UN)
            steps(act, 5, NB - 4, UN, step)
            for i in range(NB - 4, NB):
                step(i, i % UN)
            relu(NB - 1, (NB - 1) % UN)

            for b in range(GB):
                act.wait_ge(prep_t, b + 1)
                act.activation(idx[:, b * P:(b + 1) * P, :].rearrange("p g u -> p u g"),
                               psE[b % 2][:, :].rearrange("p (u g) -> p u g", u=TPG), ACT.Relu).then_inc(idx_c, 1)

            def stage_idx(g, s):
                act.wait_ge(idx_c, GB)
                if not isinstance(g, int) or g >= SLOTS:
                    act.wait_ge(grp_mm, g - (SLOTS - 1))
                act.copy(idx_now[:, s, :], idx[:, bass.ds(g, 1), :].rearrange("p g u -> p (g u)")).then_inc(idx_st, 1)
            for g in range(SLOTS):
                stage_idx(g, g)

            def own(i, s):
                if not isinstance(i, int) or i >= 2:
                    act.wait_ge(own_mm, i - 1)
                act.copy(stage[:, s % 2, 0, :], hT[:, blk(i)]).then_inc(own_st, 1)
            act.wait_ge(hT_all, NB)
            own(0, 0)
            own(1, 1)
            steps(act, 2, NB, UN, own)
            steps(act, SLOTS, G, SLOTS, stage_idx)

            def stage_acc(i, s):
                if not isinstance(i, int) or i >= 2:
                    act.wait_ge(fin_mm, i - 1)
                act.copy(stage[:, s % 2, :, :],
                         acc[:, bass.ds(i * (P * T), P * T)].rearrange("p (n t) -> p t n", t=T)).then_inc(fin_st, 1)
            act.wait_ge(own_mm, NB)
            act.wait_ge(grp_add, G)
            stage_acc(0, 0)
            stage_acc(1, 1)
            steps(act, 2, NB, UN, stage_acc)

        @block.vector
        def _(dve):
            c = [0]

            def link(ins):
                c[0] += 1
                ins.then_inc(dv, 1)
                dve.wait_ge(dv, c[0])

            dve.memset(nt_raw[:, :], 0)
            dve.memset(eps[:, :], EPS)
            dve.memset(stage[:, :, :, :], 0.0).then_inc(dv, 2)
            c[0] += 2
            dve.wait_ge(consts, 3)
            dve.tensor_scalar(ident[:, :], iota_p[:, :], iota_c[:, 0:1], None, ALU.is_equal).then_inc(ident_ok, 1)
            dve.wait_ge(small_in, 64)
            dve.tensor_copy(nt_f[:, :], nt_raw[:, :]).then_inc(types_ok, 1)
            for half in range(2):
                dve.wait_ge(x_in[half], 16 * (half + 1))
                a, b = (0, NF // 2) if half == 0 else (NF // 2, NB)

                def stat_step(i, s):
                    dve.bn_stats(stats[:, s % 2, :], xb[:, blk(i)]).then_inc(stat, 1)
                    dve.wait_ge(stat, i + 1)
                    dve.bn_aggr(mv[:, bass.ds(i, 1), :].rearrange("p b k -> p (b k)"), stats[:, s % 2, :]).then_inc(agg2, 1)
                for i in range(a, b):
                    stat_step(i, i)
            dve.wait_ge(agg2, NB)
            dve.nop().then_inc(var_ok, 1)
            dve.wait_ge(std_ok, 1)
            link(dve.reciprocal(rstd[:, :], std[:, :]))
            dve.scalar_tensor_tensor(out=nbias[:, :], in0=mv[:, :, 0], scalar=-1.0, in1=rstd[:, :],
                                     op0=ALU.mult, op1=ALU.mult).then_inc(norm_ok, 1)

            dve.wait_ge(edges_in, 16 * (3 * (GB + 1) + 1))
            dve.tensor_reduce(lo[:, :], e_dst[:, :, :], AX_X, ALU.min)
            link(dve.tensor_reduce(hi[:, :], e_dst[:, :, :], AX_X, ALU.max))
            dve.tensor_scalar(lo3[:, :], lo[:, :], float(T), None, ALU.mult)
            dve.tensor_tensor(span[:, :], hi[:, :], lo[:, :], ALU.subtract)
            link(dve.scalar_tensor_tensor(out=e_key[:, :, :], in0=e_dst[:, :, :], scalar=float(T), in1=e_typ[:, :, :],
                                          op0=ALU.mult, op1=ALU.add))
            dve.scalar_tensor_tensor(out=e_idx, in0=e_src, scalar=float(T), in1=e_typ, op0=ALU.mult, op1=ALU.add)
            for b in range(GB):
                m = dve.tensor_scalar(e_key[:, b, :], e_key[:, b, :], lo3[:, b:b + 1], None, ALU.subtract)
            m.then_inc(key_ok, 1)

            def msg_step(i, s):
                dve.wait_ge(tab_mm, i + 1)
                if not isinstance(i, int) or i >= 2:
                    dve.wait_ge(tab_msg, i - 1)
                dve.tensor_tensor(msum[:, s % 2, :], psM[s % 2][:, 0:TD], be[:, :], ALU.add).then_inc(tab_sum, 1)
                dve.tensor_copy(hT[:, blk(i)], hTs[:, s, :]).then_inc(hT_all, 1)
                dve.tensor_tensor(xb[:, blk(i)], xb[:, blk(i)], h[:, s, :], ALU.add).then_inc(xh_ok, 1)
            msg_step(0, 0)
            msg_step(1, 1)
            steps(dve, 2, NB, UN, msg_step)

            for b in range(GB):
                dve.wait_ge(prep_t, GB + b + 1)
                dve.tensor_copy(key[:, b * P:(b + 1) * P, :].rearrange("p g u -> p u g"),
                                psE[(GB + b) % 2][:, :].rearrange("p (u g) -> p u g", u=TPG)).then_inc(key_c, 1)
            dve.wait_ge(prep_t, 2 * GB + 2)
            dve.tensor_copy(ctrl[0:1, 0, :], psE[2][0:1, :]).then_inc(ctrl_ok, 1)
            link(dve.tensor_copy(span_i[:, :], psE[3][0:1, :]))
            shift = WIN.bit_length() - 1
            dve.tensor_scalar(ctrl[0:1, 1, :], span_i[:, :], shift, None, ALU.arith_shift_right).then_inc(ctrl_ok, 1)

            dve.wait_ge(w_c, T + T * NP + 1)
            for t in range(T):
                m = dve.tensor_scalar(mask[:, t, :], ntT[:, :], float(t), None, ALU.is_equal)
            link(m)

            def own(i, s):
                dve.wait_ge(own_mm, i + 1)
                dve.tensor_tensor(msum[:, s % 2, :], psM[s % 2][:, 0:TD], bn[:, :], ALU.add).then_inc(own_rd, 1)
                dve.wait_ge(own_rd, i + 1)
                for t in range(T):
                    dve.scalar_tensor_tensor(
                        out=xb[:, blk(i)], in0=msum[:, s % 2, t * D:(t + 1) * D], scalar=mask[:, t, bass.ds(i, 1)],
                        in1=xb[:, blk(i)], op0=ALU.mult, op1=ALU.add).then_inc(own_add, 1)
                    dve.wait_ge(own_add, 3 * i + (t + 1))
            dve.wait_ge(tab_msg, NB)
            dve.wait_ge(xh_ok, NB)
            own(0, 0)
            own(1, 1)
            steps(dve, 2, NB, UN, own)

            dve.wait_ge(prep_t, 2 * GB + 2)
            dve.memset(acc[:, 0:3 * EW], 0.0).then_inc(acc_zero, 1)
            dve.wait_ge(acc_zero, 2)
            dve.wait_ge(key_c, GB)
            dve.wait_ge(ctrl_ok, 2)
            passes = dve.alloc_register("passes")
            at = dve.alloc_register("at")
            dve.reg_mov(passes, 0)
            hot_shape = [P, TPG, WC]
            iota_b = iota_w[:, :].unsqueeze(1).to_broadcast(hot_shape)

            def hot(g, s):
                if not isinstance(g, int) or g >= 4:
                    dve.wait_ge(grp_mm, g - 3)
                dve.tensor_tensor(onehot[:, s % 4, :, :], iota_b,
                                  key[:, bass.ds(g, 1), :].rearrange("p g u -> p (g u)").unsqueeze(2)
                                  .to_broadcast(hot_shape), ALU.is_equal).then_inc(hot_ok, 1)

            def add(g, s):
                more = dve.value_load(ctrl[0:1, 1, bass.ds(g, 1)], min_val=0, max_val=N // WIN)
                col = dve.value_load(ctrl[0:1, 0, bass.ds(g, 1)], min_val=0, max_val=(N - 1) * T)
                with dve.If(more > 0):
                    dve.tensor_copy(key_x[:, 0, :], key[:, bass.ds(g, 1), :].rearrange("p g u -> p (g u)"))
                    dve.reg_mov(at, col)
                    with dve.Fori(0, more) as _k:
                        if not isinstance(g, int) or g >= 1:
                            dve.wait_ge(grp_add, g)
                        dve.reg_add(passes, passes, 1)
                        n = dve.snap(passes, min_val=1)
                        dve.drain()
                        dve.tensor_scalar(key_x[:, 1, :], key_x[:, 0, :], float(WC), None, ALU.subtract).then_inc(xkey, 1)
                        dve.wait_ge(xkey, n)
                        dve.tensor_copy(key_x[:, 0, :], key_x[:, 1, :])
                        dve.tensor_tensor(onehot_x[:, :, :], iota_b, key_x[:, 1, :].unsqueeze(2).to_broadcast(hot_shape),
                                          ALU.is_equal).then_inc(xhot_ok, 1)
                        dve.wait_ge(x_mm, n)
                        dve.reg_add(at, at, WC)
                        there = acc[:, bass.ds(dve.snap(at, min_val=0, max_val=AW - WC), WC)]
                        dve.tensor_tensor(there, psT[0][:, 0:WC], there, ALU.add).then_inc(x_add, 1)
                        dve.wait_ge(x_add, n)
                if not isinstance(g, int) or g >= 1:
                    dve.wait_ge(grp_add, g)
                dve.wait_ge(grp_mm, g + 1)
                there = acc[:, bass.ds(col, WC)]
                dve.tensor_tensor(there, psE[s % 4][:, 0:WC], there, ALU.add).then_inc(grp_add, 1)

            def edge_step(g, s):
                if not isinstance(g, int) or g + 1 < G:
                    hot(g + 1, (s + 1) % SLOTS)
                add(g, s)
            hot(0, 0)
            for g in range(SLOTS):
                edge_step(g, g)
            steps(dve, SLOTS, G - 3, SLOTS, edge_step)
            for g in range(G - 3, G):
                edge_step(g, g % SLOTS)

            def finish(i, s):
                dve.wait_ge(fin_mm, i + 1)
                if not isinstance(i, int) or i >= 4:
                    dve.wait_ge(fin_out[s], (i - s) * (16 // UN))
                for t in range(T):
                    ins = dve.scalar_tensor_tensor(
                        out=(xb[:, blk(i)] if t < T - 1 else fin[:, s, 0:D]), in0=psM[s % 2][:, t * D:(t + 1) * D],
                        scalar=mask[:, t, bass.ds(i, 1)], in1=xb[:, blk(i)], op0=ALU.mult, op1=ALU.add)
                    ins.then_inc(fin_acc if t == T - 1 else own_add, 1)
                    if t < T - 1:
                        dve.wait_ge(own_add, 2 * i + (3 * NB + t + 1))
                    else:
                        dve.wait_ge(fin_acc, i + 1)
                        dve.nop().then_inc(fin_ok, 1)
            for i in range(4):
                finish(i, i)
            steps(dve, 4, NB, UN, finish)


_INS = ["x", "src", "dst", "edge_type_3", "node_type_3", "L0_gnn_W_e", "L0_gnn_b_e", "L0_gnn_W_n", "L0_gnn_b_n"]


def kernel(**inputs):
    import numpy as _np
    import concourse.bacc as _bacc
    from concourse import mybir as _mybir
    from concourse.bass_utils import run_bass_kernel_spmd as _run

    nc = _bacc.Bacc("TRN2", target_bir_lowering=False, num_devices=1)
    arrays, args = {}, []
    for name in _INS:
        a = _np.ascontiguousarray(inputs[name])
        arrays[f"in_{name}_dram"] = a
        args.append(nc.dram_tensor(f"in_{name}_dram", a.shape, _mybir.dt.from_np(a.dtype), kind="ExternalInput").ap())
    shape = _np.shape(inputs["x"])
    out = nc.dram_tensor("out_dram", shape, _mybir.dt.float32, kind="ExternalOutput").ap()
    build(nc, *args, out)
    r = _run(nc, [arrays], core_ids=[0])
    return r.results[0]["out_dram"]
```

```python
import concourse.bass as bass
from concourse import mybir
from contextlib import ExitStack

F32 = mybir.dt.float32
I32 = mybir.dt.int32
ALU = mybir.AluOpType
ACT = mybir.ActivationFunctionType
AX_X = mybir.AxisListType.X

P = 128
T = 3
EPS = 1e-5
TPG = 4
GE = TPG * P
SLOTS = 8
WIN = 32
WC = WIN * T
PAD_TYPE = -100000
UN = 4
BF16 = mybir.dt.bfloat16
CHUNKS = (8, 24)
FAR = 1 << 20


def build(nc, x, src, dst, etype, ntype, w_e, b_e, w_n, b_n, out):
    N, D = x.shape
    E = src.shape[0]
    NB = -(-N // P)
    NF = N // P
    NR = N - NF * P
    G = -(-E // GE)
    GF = E // GE
    ER = E - GF * GE
    GB = -(-G // P)
    TD = T * D
    AW = max(N + WIN, NB * P) * T
    NP = D // P + T
    IT = G // SLOTS
    MB = 64
    PB = P.bit_length() - 1
    assert NB <= IT < MB and MB * SLOTS == GB * P
    assert D == P and NR and ER and NB % UN == 1 and GF < GB * P

    table = nc.dram_tensor("message_table", [N, TD], F32, kind="Internal").ap()
    table_rows = table.rearrange("n (t d) -> (n t) d", t=T)

    with ExitStack() as ctx:
        def sb(name, shape, dt=F32):
            return ctx.enter_context(nc.sbuf_tensor(name, shape, dt))

        def sem(name):
            return ctx.enter_context(nc.semaphore(name))

        acc = sb("acc", [P, AW])
        xb = sb("xb", [P, NB * D])
        rows = sb("rows", [P, SLOTS, TPG, D])
        onehot = sb("onehot", [P, 4, TPG, WC])
        onehot_x = sb("onehot_x", [P, TPG, WC])
        iota_w = sb("iota_w", [P, WC])
        iota_p = sb("iota_p", [P, P])
        iota_c = sb("iota_c", [P, 1])
        ident = sb("ident", [P, P])
        EW = GB * GE
        e_src, e_dst, e_typ = (acc[:, k * EW:(k + 1) * EW].rearrange("p (b j) -> p b j", b=GB).bitcast(I32)
                               for k in range(3))
        e_idx, e_key = (acc[:, k * EW:(k + 1) * EW].rearrange("p (b j) -> p b j", b=GB) for k in range(2))
        lo = sb("lo", [P, GB])
        hi = sb("hi", [P, GB])
        lo3 = sb("lo3", [P, GB])
        span = sb("span", [P, GB])
        idx = sb("idx", [P, GB * P, TPG], I32)
        key = sb("key", [P, GB * P, TPG])
        idx_now = sb("idx_now", [P, SLOTS, TPG], I32)
        key_x = sb("key_x", [P, 2, TPG])
        ctrl = sb("ctrl", [1, 2, GB * P], I32)
        span_i = sb("span_i", [1, GB * P], I32)
        ahead = sb("ahead", [1, 2, 2 * MB])
        ahead_i = sb("ahead_i", [1, 2, MB], I32)
        upto = sb("upto", [1, MB], I32)
        we_raw = sb("we_raw", [P, T, D])
        wn_raw = sb("wn_raw", [P, T, NP * D])
        weT = sb("weT", [P, TD])
        wnT = sb("wnT", [P, NP, TD])
        be = sb("be", [T, TD])
        be_p = sb("be_p", [T, 2, TD])
        be_h = sb("be_h", [T, 3, TD], BF16)
        be_3 = sb("be_3", [T, TD], BF16)
        ones = sb("ones", [T, P], BF16)
        pick = sb("pick", [T, 3])
        bn = sb("bn", [P, TD])
        nt_raw = sb("nt_raw", [P, P], I32)
        nt_f = sb("nt_f", [P, P])
        ntT = sb("ntT", [P, NB])
        mask = sb("mask", [P, T, NB])
        stats = sb("stats", [P, 4, 6])
        mv = sb("mv", [P, NB, 2])
        std = sb("std", [P, NB])
        rstd = sb("rstd", [P, NB])
        nbias = sb("nbias", [P, NB])
        eps = sb("eps", [P, 1])
        h = sb("h", [P, 4, D])
        hT = sb("hT", [P, 4, P])
        msg = sb("msg", [P, 4, TD])
        h_own = sb("h_own", [P, D])
        hT_own = sb("hT_own", [P, P])
        own_sum = sb("own_sum", [P, TD])
        stage = sb("stage", [P, T, P])

        psT = [ctx.enter_context(nc.psum_tensor(f"psT{i}", [P, 512], F32)) for i in range(2)]
        psM = [ctx.enter_context(nc.psum_tensor(f"psM{i}", [P, 512], F32)) for i in range(2)]
        psE = [ctx.enter_context(nc.psum_tensor(f"psE{i}", [P, 512], F32)) for i in range(4)]
        psH = [psM[0], psM[1], psE[2], psE[3]]

        edges_in = sem("edges_in")
        x_in = [sem(f"x_in{i}") for i in range(3)]
        we_in = sem("we_in")
        wn_in = sem("wn_in")
        be_in = sem("be_in")
        small_in = sem("small_in")
        zeroed = sem("zeroed")
        consts = sem("consts")
        ident_ok = sem("ident_ok")
        types_ok = sem("types_ok")
        bias_ok = sem("bias_ok")
        pads = sem("pads")
        xpad = sem("xpad")
        acc_zero = sem("acc_zero")
        idx_i = sem("idx_i")
        idx_f = sem("idx_f")
        dv = sem("dv")
        w_t = sem("w_t")
        w_c = sem("w_c")
        stat = sem("stat")
        var_ok = sem("var_ok")
        std_ok = sem("std_ok")
        norm_ok = sem("norm_ok")
        key_ok = sem("key_ok")
        idx_t = sem("idx_t")
        idx_c = sem("idx_c")
        key_t = sem("key_t")
        key_c = sem("key_c")
        ctl_t = sem("ctl_t")
        ctrl_ok = sem("ctrl_ok")
        h_ok = sem("h_ok")
        h_t = sem("h_t")
        hT_ok = sem("hT_ok")
        tab_mm = sem("tab_mm")
        tab_msg = [sem(f"tab_msg{i}") for i in range(4)]
        tab_out = [sem(f"tab_out{i}") for i in range(4)]
        idx_st = sem("idx_st")
        landed = [sem(f"landed{i}") for i in range(SLOTS)]
        hot_ok = sem("hot_ok")
        grp_mm = sem("grp_mm")
        grp_add = sem("grp_add")
        xkey = sem("xkey")
        xhot_ok = sem("xhot_ok")
        x_mm = sem("x_mm")
        x_add = sem("x_add")
        own_h = sem("own_h")
        own_t = sem("own_t")
        own_st = sem("own_st")
        own_mm = sem("own_mm")
        own_rd = sem("own_rd")
        own_add = sem("own_add")
        fin_st = sem("fin_st")
        fin_mm = sem("fin_mm")
        fin_part = sem("fin_part")
        fin_ok = sem("fin_ok")
        fin_out = sem("fin_out")

        def blk(i):
            return bass.ds(i * D, D)

        def later(i, first=1):
            return not isinstance(i, int) or i >= first

        def in_order(i):
            return not isinstance(i, int) or i < NB

        def steps(eng, first, last, unroll, step):
            loops = (last - first) // unroll
            if loops > 1:
                with eng.Fori(0, loops) as r:
                    for s in range(unroll):
                        step(r * unroll + (first + s), (first + s) % unroll)
                first += loops * unroll
            for i in range(first, last):
                step(i, i % unroll)

        CUTS = (0,) + CHUNKS + (NB,)
        block = ctx.enter_context(nc.Block())

        @block.sync
        def _(sp):
            for c in range(3):
                a, b = CUTS[c], min(CUTS[c + 1], NF)
                sp.dma_start(xb[:, a * D:b * D],
                             x[a * P:b * P, :].rearrange("(b p) d -> p b d", p=P)).then_inc(x_in[c], 16)
            sp.wait_ge(xpad, 1)
            sp.dma_start(xb[0:NR, NF * D:NB * D], x[NF * P:N, :]).then_inc(x_in[2], 16)
            sp.wait_ge(pads, 3)
            for a, e0 in ((e_src, src), (e_typ, etype), (e_dst, dst)):
                for b in range(GB):
                    n = min(P, GF - b * P)
                    sp.dma_start(a[0:n, b, :], e0[b * P * GE:(b * P + n) * GE]
                                 .rearrange("(r j) -> r j", j=GE)).then_inc(edges_in, 16)
                r, b = GF % P, GF // P
                sp.dma_start(a[r:r + 1, b, 0:ER],
                             e0[GF * GE:E].rearrange("(r j) -> r j", r=1)).then_inc(edges_in, 16)
            sp.dma_start(e_dst[GF % P:GF % P + 1, GF // P, ER:GE],
                         dst[E - (GE - ER):E].rearrange("(r j) -> r j", r=1)).then_inc(edges_in, 16)

            with sp.Fori(0, NF // UN) as r:
                for s in range(UN):
                    sp.wait_ge(tab_msg[s], r + 1)
                    sp.dma_start(table[bass.ds(r * (UN * P) + s * P, P), :], msg[:, s, :]).then_inc(tab_out[s], 16)
            sp.wait_ge(tab_msg[0], NF // UN + 1)
            sp.dma_start(table[NF * P:N, :], msg[0:NR, 0, :]).then_inc(tab_out[0], 16)

            with sp.Fori(0, NF) as i:
                sp.wait_ge(fin_ok, i + 2)
                sp.dma_start(out[bass.ds(i * P, P), :], xb[:, blk(i)]).then_inc(fin_out, 16)
            sp.wait_ge(fin_ok, NB + 1)
            sp.dma_start(out[NF * P:N, :], xb[0:NR, blk(NF)]).then_inc(fin_out, 16)
            sp.wait_ge(fin_out, 16 * NB)

        @block.gpsimd
        def _(pool):
            pool.iota(iota_p[:, :], [[1, P]], base=0, channel_multiplier=0,
                      allow_small_or_imprecise_dtypes=True).then_inc(consts, 1)
            pool.iota(iota_c[:, :], [[0, 1]], base=0, channel_multiplier=1,
                      allow_small_or_imprecise_dtypes=True).then_inc(consts, 1)
            pool.memset(xb[:, NF * D:NB * D], 0.0).then_inc(xpad, 1)
            pool.memset(e_src[:, GB - 1, :], 0).then_inc(pads, 1)
            pool.memset(e_typ[:, GB - 1, :], PAD_TYPE).then_inc(pads, 1)
            pool.memset(e_dst[:, GB - 1, :], FAR).then_inc(pads, 1)
            pool.iota(iota_w[:, :], [[1, WC]], base=0, channel_multiplier=0,
                      allow_small_or_imprecise_dtypes=True).then_inc(consts, 1)
            pool.memset(acc[:, 3 * EW:AW], 0.0).then_inc(acc_zero, 1)
            pool.wait_ge(edges_in, 16 * (3 * (GB + 1) + 1))
            pool.tensor_scalar(e_src, e_src, float(T), None, ALU.mult).then_inc(idx_i, 1)
            pool.wait_ge(idx_i, 1)
            pool.tensor_tensor(e_src, e_src, e_typ, ALU.add).then_inc(idx_i, 1)
            for s in range(UN):
                pool.wait_ge(tab_out[s], 16 * len(range(s, NB, UN)))
            due = pool.alloc_register("due")
            pool.reg_mov(due, 1)

            def gather(g, s):
                if isinstance(g, int):
                    pool.wait_ge(idx_st, g + 1)
                else:
                    pool.wait_ge(idx_st, pool.snap(due, min_val=1))
                    pool.reg_add(due, due, 1)
                for u in range(TPG):
                    pool.indirect_dma_start(
                        out=rows[:, s, u, :], out_offset=None, in_=table_rows,
                        in_offset=bass.IndirectOffsetOnAxis(ap=idx_now[:, s, u:u + 1], axis=0),
                    ).then_inc(landed[s], 16)
            steps(pool, 0, G, SLOTS, gather)

        @block.tensor
        def _(pe):
            pe.sem_inc(fin_mm, 1)
            n = [0]

            def weight(a):
                if n[0] >= 2:
                    pe.wait_ge(w_c, n[0] - 1)
                pe.transpose(psT[n[0] % 2][:, 0:P], a, ident[:, :]).then_inc(w_t, 1)
                n[0] += 1

            pe.wait_ge(ident_ok, 1)
            pe.wait_ge(we_in, 16)
            for t in range(T):
                weight(we_raw[:, t, :])
            pe.wait_ge(bias_ok, 1)

            def tr(i, s):
                pe.wait_ge(h_ok, i + 1)
                pe.transpose(psT[s % 2][:, 0:P], h[:, s, :], ident[:, :]).then_inc(h_t, 1)

            def mm(i, s, turn):
                if turn is not None:
                    pe.wait_ge(tab_msg[s], turn)
                pe.matmul(psH[s][:, 0:TD], ones[:, :], be_3[:, :], start=True, stop=False)
                pe.wait_ge(hT_ok, i + 1)
                pe.matmul(psH[s][:, 0:TD], hT[:, s, :], weT[:, :], start=False, stop=True).then_inc(tab_mm, 1)

            pe.wait_ge(w_c, n[0])
            tr(0, 0)
            for i in range(UN):
                tr(i + 1, (i + 1) % UN)
                mm(i, i, None)
            with pe.Fori(1, NF // UN) as r:
                for s in range(UN):
                    tr(r * UN + (s + 1), (s + 1) % UN)
                    mm(r * UN + s, s, r)
            mm(NF, 0, NF // UN)

            pe.wait_ge(idx_f, 1)
            for b in range(GB):
                if b >= 2:
                    pe.wait_ge(idx_c, b - 1)
                for u in range(TPG):
                    m = pe.transpose(psE[b % 2][:, u * P:(u + 1) * P], e_idx[:, b, u * P:(u + 1) * P], ident[:, :])
                m.then_inc(idx_t, 1)
            pe.wait_ge(key_ok, 1)
            for b in range(GB):
                if b >= 2:
                    pe.wait_ge(key_c, b - 1)
                else:
                    pe.wait_ge(idx_c, GB - 1 + b)
                for u in range(TPG):
                    m = pe.transpose(psE[b % 2][:, u * P:(u + 1) * P], e_key[:, b, u * P:(u + 1) * P], ident[:, :])
                m.then_inc(key_t, 1)
            for s in (2, 3):
                pe.wait_ge(tab_msg[s], NF // UN)
            for a, q in ((lo, 2), (span, 3)):
                for b in range(GB):
                    m = pe.matmul(psE[q][0:1, b * P:(b + 1) * P], a[:, b:b + 1], ident[:, :], start=True, stop=True)
                m.then_inc(ctl_t, 1)

            pe.wait_ge(wn_in, 16)
            for t in range(T):
                for p in range(NP):
                    weight(wn_raw[:, t, p * D:(p + 1) * D])
            pe.wait_ge(types_ok, 1)
            weight(nt_f[:, :])

            pe.wait_ge(key_c, GB)
            pe.wait_ge(ctrl_ok, 1)
            pe.wait_ge(w_c, n[0])
            for s in (0, 1):
                pe.wait_ge(tab_msg[s], NF // UN)
            pe.wait_ge(tab_msg[0], NF // UN + 1)
            passes = pe.alloc_register("passes")
            pe.reg_mov(passes, 0)
            done = pe.alloc_register("done")
            pe.reg_mov(done, 0)

            def group(g, s):
                more = pe.value_load(ctrl[0:1, 1, bass.ds(g, 1)], min_val=0, max_val=N // WIN)
                turn = g // SLOTS + 1 if isinstance(g, int) else None
                pe.wait_ge(landed[s], 16 * TPG * turn if turn else (g - s) * (16 * TPG // SLOTS) + 16 * TPG)
                with pe.If(more > 0):
                    with pe.Fori(0, more) as _k:
                        pe.reg_add(passes, passes, 1)
                        pe.wait_ge(xhot_ok, pe.snap(passes, min_val=1))
                        for u in range(TPG):
                            m = pe.matmul(psT[0][:, 0:WC], rows[:, s, u, :], onehot_x[:, u, :],
                                          start=(u == 0), stop=(u == TPG - 1))
                        m.then_inc(x_mm, 1)
                pe.wait_ge(hot_ok, g + 1)
                if later(g, 4):
                    pe.wait_ge(grp_add, g - 3)
                for u in range(TPG):
                    m = pe.matmul(psE[s % 4][:, 0:WC], rows[:, s, u, :], onehot[:, s % 4, u, :],
                                  start=(u == 0), stop=(u == TPG - 1))
                m.then_inc(grp_mm, 1)

            def own_tr(i):
                pe.wait_ge(own_h, i + 1)
                pe.transpose(psT[1][:, 0:P], h_own[:, :], ident[:, :]).then_inc(own_t, 1)

            def own_mul(i):
                pe.wait_ge(own_st, i + 1)
                if later(i):
                    pe.wait_ge(own_rd, i)
                pe.matmul(psM[0][:, 0:TD], hT_own[:, :], wnT[:, 0, :], start=True, stop=True).then_inc(own_mm, 1)

            def finish(i):
                pe.wait_ge(fin_st, i + 1)
                pe.wait_ge(fin_ok, i + 1)
                for t in range(T):
                    m = pe.matmul(psM[1][:, 0:TD], stage[:, t, :], wnT[:, 1 + t, :], start=(t == 0), stop=(t == T - 1))
                m.then_inc(fin_mm, 1)

            def finish_to(end, always):
                if always:
                    with pe.Fori(pe.snap(done, min_val=0, max_val=NB - 1), end) as i:
                        finish(i)
                    return
                with pe.If(end > pe.snap(done, min_val=0, max_val=NB - 1)):
                    with pe.Fori(pe.snap(done, min_val=0, max_val=NB - 1), end) as i:
                        finish(i)
                    pe.reg_mov(done, end)

            def round_(r):
                for s in range(SLOTS):
                    group(r * SLOTS + s, s)
                    if s == 2 and in_order(r):
                        own_tr(r)
                    if s == 5 and in_order(r):
                        own_mul(r)
                    if s == 7 and later(r):
                        finish_to(pe.value_load(upto[0:1, bass.ds(r - 1, 1)], min_val=0, max_val=NF), False)
            round_(0)
            with pe.Fori(1, NB) as r:
                round_(r)
            for r in range(NB, IT):
                round_(r)
            for g in range(IT * SLOTS, G):
                group(g, g % SLOTS)
            finish_to(NB, True)

        @block.scalar
        def _(act):
            act.dma_start(be[:, :], b_e.rearrange("(a t) o -> a (t o)", a=1).to_broadcast([T, TD])).then_inc(be_in, 16)
            act.dma_start(we_raw[:, :, :], w_e.rearrange("t o i -> o t i")).then_inc(we_in, 16)
            act.dma_start(wn_raw[:, :, :], w_n.rearrange("t o i -> o t i")).then_inc(wn_in, 16)
            act.wait_ge(zeroed, 1)
            act.dma_start(nt_raw[0:NF, :], ntype[0:NF * P].rearrange("(b p) -> b p", p=P)).then_inc(small_in, 16)
            act.dma_start(nt_raw[NF:NB, 0:NR], ntype[NF * P:N].rearrange("(b p) -> b p", b=1)).then_inc(small_in, 16)
            act.dma_start(bn[:, :], b_n.rearrange("(a t) o -> a (t o)", a=1).to_broadcast([P, TD])).then_inc(small_in, 16)
            n = [0]

            def weight(o, a):
                act.wait_ge(w_t, n[0] + 1)
                act.copy(o, psT[n[0] % 2][:, 0:a]).then_inc(w_c, 1)
                n[0] += 1

            def deviations(c):
                a, b = CUTS[c], CUTS[c + 1]
                act.wait_ge(var_ok, c + 1)
                act.activation(std[:, a:b], mv[:, a:b, 1], ACT.Sqrt, bias=eps[:, 0:1]).then_inc(std_ok, 1)

            def norm_into(o, i):
                return act.activation(o, xb[:, blk(i)], ACT.Relu, scale=rstd[:, bass.ds(i, 1)],
                                      bias=nbias[:, bass.ds(i, 1)])

            def norm(i, s):
                norm_into(h[:, s, :], i).then_inc(h_ok, 1)

            def copy_t(i, s):
                act.wait_ge(h_t, i + 1)
                if later(i, 4):
                    act.wait_ge(tab_mm, i - 3)
                act.copy(hT[:, s, :], psT[s % 2][:, 0:P]).then_inc(hT_ok, 1)

            def relu(i, s):
                act.wait_ge(tab_mm, i + 1)
                if later(i, UN):
                    act.wait_ge(tab_out[s], (i - s) * (16 // UN))
                act.activation(msg[:, s, :], psH[s][:, 0:TD], ACT.Relu).then_inc(tab_msg[s], 1)

            def step(i, s):
                if in_order(i + 1 if isinstance(i, int) else 0):
                    norm(i + 1, (s + 1) % UN)
                copy_t(i, s)
                if s % 2 == 1:
                    relu(i - 1, s - 1)
            deviations(0)
            for t in range(T):
                weight(weT[:, t * D:(t + 1) * D], P)
            act.wait_ge(norm_ok, 1)
            norm(0, 0)
            a = CHUNKS[0] - 1
            for i in range(a):
                step(i, i % UN)
            deviations(1)
            act.wait_ge(norm_ok, 2)
            b = CHUNKS[1] - 1
            steps(act, a, b, UN, step)
            deviations(2)
            act.wait_ge(norm_ok, 3)
            act.wait_ge(idx_i, 2)
            act.activation(e_idx, e_src, ACT.Relu).then_inc(idx_f, 1)
            steps(act, b, NB - 1, UN, step)
            step(NB - 1, (NB - 1) % UN)
            relu(NB - 1, (NB - 1) % UN)

            for b in range(GB):
                act.wait_ge(idx_t, b + 1)
                act.copy(idx[:, b * P:(b + 1) * P, :].rearrange("p g u -> p u g"),
                         psE[b % 2][:, :].rearrange("p (u g) -> p u g", u=TPG)).then_inc(idx_c, 1)

            def stage_idx(g, s):
                if later(g, SLOTS):
                    act.wait_ge(grp_mm, g - (SLOTS - 1))
                act.copy(idx_now[:, s, :], idx[:, bass.ds(g, 1), :].rearrange("p g u -> p (g u)")).then_inc(idx_st, 1)
            act.wait_ge(idx_c, GB)
            for g in range(SLOTS):
                stage_idx(g, g)
            for t in range(T):
                for p in range(NP):
                    weight(wnT[:, p, t * D:(t + 1) * D], P)
            weight(ntT[:, :], NB)

            done = act.alloc_register("done")
            act.reg_mov(done, 0)

            def own_norm(i):
                if later(i):
                    act.wait_ge(own_add, 4 * i - 3)
                norm_into(h_own[:, :], i).then_inc(own_h, 1)

            def own_copy(i):
                act.wait_ge(own_t, i + 1)
                if later(i):
                    act.wait_ge(own_mm, i)
                act.copy(hT_own[:, :], psT[1][:, 0:P]).then_inc(own_st, 1)

            def finish(i):
                act.wait_ge(fin_mm, i + 1)
                act.copy(stage[:, :, :],
                         acc[:, bass.ds(i * (P * T), P * T)].rearrange("p (n t) -> p t n", t=T)).then_inc(fin_st, 1)

            def finish_to(end, always):
                if always:
                    with act.Fori(act.snap(done, min_val=0, max_val=NB - 1), end) as i:
                        finish(i)
                    return
                with act.If(end > act.snap(done, min_val=0, max_val=NB - 1)):
                    with act.Fori(act.snap(done, min_val=0, max_val=NB - 1), end) as i:
                        finish(i)
                    act.reg_mov(done, end)

            def round_(r):
                last = isinstance(r, int) and r >= IT - 1
                for s in range(SLOTS):
                    if not last or (r + 1) * SLOTS + s < G:
                        stage_idx((r + 1) * SLOTS + s, s)
                    if s == 0 and in_order(r):
                        own_norm(r)
                    if s == 3 and in_order(r):
                        own_copy(r)
                    if s == 5 and later(r):
                        act.wait_ge(grp_add, r * SLOTS)
                        finish_to(act.value_load(upto[0:1, bass.ds(r - 1, 1)], min_val=0, max_val=NF), False)
            act.wait_ge(ctrl_ok, 1)
            round_(0)
            with act.Fori(1, NB) as r:
                round_(r)
            for r in range(NB, IT):
                round_(r)
            act.wait_ge(grp_add, G)
            finish_to(NB, True)

        @block.vector
        def _(dve):
            c = [0]

            def link(ins):
                c[0] += 1
                ins.then_inc(dv, 1)
                dve.wait_ge(dv, c[0])

            dve.sem_inc(fin_ok, 1)
            dve.memset(nt_raw[:, :], 0).then_inc(zeroed, 1)
            dve.memset(eps[:, :], EPS)
            dve.memset(ones[:, :], 1.0)
            for k in range(2):
                link(dve.memset(ahead[:, k, :], float(FAR)))
            dve.wait_ge(consts, 2)
            dve.tensor_scalar(ident[:, :], iota_p[:, :], iota_c[:, 0:1], None, ALU.is_equal).then_inc(ident_ok, 1)
            for k in range(3):
                link(dve.tensor_scalar(pick[:, k:k + 1], iota_c[0:T, 0:1], float(k), None, ALU.is_equal))
            dve.wait_ge(be_in, 16)
            link(dve.tensor_copy(be_h[:, 0, :], be[:, :]))
            link(dve.tensor_tensor(be_p[:, 0, :], be[:, :], be_h[:, 0, :], ALU.subtract))
            link(dve.tensor_copy(be_h[:, 1, :], be_p[:, 0, :]))
            link(dve.tensor_tensor(be_p[:, 1, :], be_p[:, 0, :], be_h[:, 1, :], ALU.subtract))
            link(dve.tensor_copy(be_h[:, 2, :], be_p[:, 1, :]))
            link(dve.tensor_scalar(be_3[:, :], be_h[:, 0, :], pick[:, 0:1], None, ALU.mult))
            link(dve.scalar_tensor_tensor(out=be_3[:, :], in0=be_h[:, 1, :], scalar=pick[:, 1:2], in1=be_3[:, :],
                                          op0=ALU.mult, op1=ALU.add))
            dve.scalar_tensor_tensor(out=be_3[:, :], in0=be_h[:, 2, :], scalar=pick[:, 2:3], in1=be_3[:, :],
                                     op0=ALU.mult, op1=ALU.add).then_inc(bias_ok, 1)

            def sums(i):
                dve.bn_stats(stats[:, i % 4, :], xb[:, i * D:(i + 1) * D]).then_inc(stat, 1)

            def moments(i):
                dve.wait_ge(stat, i + 1)
                return dve.bn_aggr(mv[:, i, :], stats[:, i % 4, :])

            def chunk_stats(a, b):
                sums(a)
                for i in range(a, b):
                    if i + 1 < b:
                        sums(i + 1)
                    m = moments(i)
                m.then_inc(var_ok, 1)

            def inverses(k):
                a, b = CUTS[k], CUTS[k + 1]
                dve.wait_ge(std_ok, k + 1)
                link(dve.reciprocal(rstd[:, a:b], std[:, a:b]))
                dve.scalar_tensor_tensor(out=nbias[:, a:b], in0=mv[:, a:b, 0], scalar=-1.0, in1=rstd[:, a:b],
                                         op0=ALU.mult, op1=ALU.mult).then_inc(norm_ok, 1)

            def relu(i, s):
                dve.wait_ge(tab_mm, i + 1)
                if later(i, UN):
                    dve.wait_ge(tab_out[s], (i - s) * (16 // UN))
                dve.tensor_scalar(msg[:, s, :], psH[s][:, 0:TD], 0.0, None, ALU.max).then_inc(tab_msg[s], 1)

            for k in range(2):
                dve.wait_ge(x_in[k], 16)
                chunk_stats(CUTS[k], CUTS[k + 1])
                inverses(k)
            dve.wait_ge(x_in[2], 32)
            i, last = CUTS[2], CUTS[3]
            sums(i)
            for j in range(1, CHUNKS[1] - 4, 2):
                relu(j, j % UN)
                for _ in range(3):
                    if i < last:
                        if i + 1 < last:
                            sums(i + 1)
                        m = moments(i)
                        i += 1
                        if i == last:
                            m.then_inc(var_ok, 1)
            inverses(2)
            j0 = CHUNKS[1] - 4 + 1
            with dve.Fori(0, (NF - j0 + 1) // UN) as r:
                for s in (1, 3):
                    relu(r * UN + (j0 + s - 1), s)

            dve.wait_ge(edges_in, 16 * (3 * (GB + 1) + 1))
            dve.tensor_reduce(lo[:, :], e_dst, AX_X, ALU.min)
            link(dve.tensor_reduce(hi[:, :], e_dst, AX_X, ALU.max))
            dve.tensor_scalar(lo3[:, :], lo[:, :], float(T), None, ALU.mult)
            dve.tensor_tensor(span[:, :], hi[:, :], lo[:, :], ALU.subtract)
            link(dve.scalar_tensor_tensor(out=e_key, in0=e_dst, scalar=float(T), in1=e_typ, op0=ALU.mult, op1=ALU.add))
            for b in range(GB):
                m = dve.tensor_scalar(e_key[:, b, :], e_key[:, b, :], lo3[:, b:b + 1], None, ALU.subtract)
            m.then_inc(key_ok, 1)
            dve.wait_ge(small_in, 48)
            dve.tensor_copy(nt_f[:, :], nt_raw[:, :]).then_inc(types_ok, 1)
            for b in range(GB):
                dve.wait_ge(key_t, b + 1)
                dve.tensor_copy(key[:, b * P:(b + 1) * P, :].rearrange("p g u -> p u g"),
                                psE[b % 2][:, :].rearrange("p (u g) -> p u g", u=TPG)).then_inc(key_c, 1)

            dve.wait_ge(ctl_t, 2)
            dve.tensor_scalar(ctrl[0:1, 0, :], psE[2][0:1, :], float(T), None, ALU.mult)
            dve.tensor_reduce(ahead[:, 0, 0:MB], psE[2][0:1, :].rearrange("p (r s) -> p r s", s=SLOTS), AX_X, ALU.min)
            link(dve.tensor_copy(span_i[:, :], psE[3][0:1, :]))
            dve.tensor_scalar(ctrl[0:1, 1, :], span_i[:, :], WIN.bit_length() - 1, None, ALU.arith_shift_right)
            q, d = 0, 1
            while d < MB:
                link(dve.tensor_tensor(ahead[:, 1 - q, 0:MB], ahead[:, q, 0:MB], ahead[:, q, d:MB + d], ALU.min))
                q, d = 1 - q, 2 * d
            link(dve.tensor_copy(ahead_i[:, 0, :], ahead[:, q, 1:MB + 1]))
            link(dve.tensor_scalar(ahead_i[:, 1, :], ahead_i[:, 0, :], PB, None, ALU.arith_shift_right))
            dve.tensor_tensor(upto[:, :], ahead_i[:, 1, :], iota_p[0:1, 1:MB + 1], ALU.min).then_inc(ctrl_ok, 1)

            dve.memset(acc[:, 0:3 * EW], 0.0).then_inc(acc_zero, 1)
            dve.wait_ge(w_c, T + T * NP + 1)
            for t in range(T):
                m = dve.tensor_scalar(mask[:, t, :], ntT[:, :], float(t), None, ALU.is_equal)
            link(m)

            dve.wait_ge(consts, 3)
            dve.wait_ge(acc_zero, 2)
            dve.wait_ge(key_c, GB)
            dve.wait_ge(ctrl_ok, 1)
            passes = dve.alloc_register("passes")
            at = dve.alloc_register("at")
            done = dve.alloc_register("done")
            dve.reg_mov(passes, 0)
            dve.reg_mov(done, 0)
            hot_shape = [P, TPG, WC]
            iota_b = iota_w[:, :].unsqueeze(1).to_broadcast(hot_shape)

            def keys_of(g):
                return key[:, bass.ds(g, 1), :].rearrange("p g u -> p (g u)")

            def hot(g, s):
                if later(g, 4):
                    dve.wait_ge(grp_mm, g - 3)
                dve.tensor_tensor(onehot[:, s % 4, :, :], iota_b, keys_of(g).unsqueeze(2).to_broadcast(hot_shape),
                                  ALU.is_equal).then_inc(hot_ok, 1)

            def add(g, s):
                more = dve.value_load(ctrl[0:1, 1, bass.ds(g, 1)], min_val=0, max_val=N // WIN)
                col = dve.value_load(ctrl[0:1, 0, bass.ds(g, 1)], min_val=0, max_val=(N - 1) * T)
                with dve.If(more > 0):
                    dve.tensor_copy(key_x[:, 0, :], keys_of(g))
                    dve.reg_mov(at, col)
                    with dve.Fori(0, more) as _k:
                        if later(g):
                            dve.wait_ge(grp_add, g)
                        dve.reg_add(passes, passes, 1)
                        n = dve.snap(passes, min_val=1)
                        dve.drain()
                        dve.tensor_scalar(key_x[:, 1, :], key_x[:, 0, :], float(WC), None, ALU.subtract).then_inc(xkey, 1)
                        dve.wait_ge(xkey, n)
                        dve.tensor_copy(key_x[:, 0, :], key_x[:, 1, :])
                        dve.tensor_tensor(onehot_x[:, :, :], iota_b, key_x[:, 1, :].unsqueeze(2).to_broadcast(hot_shape),
                                          ALU.is_equal).then_inc(xhot_ok, 1)
                        dve.wait_ge(x_mm, n)
                        dve.reg_add(at, at, WC)
                        there = acc[:, bass.ds(dve.snap(at, min_val=0, max_val=AW - WC), WC)]
                        dve.tensor_tensor(there, psT[0][:, 0:WC], there, ALU.add).then_inc(x_add, 1)
                        dve.wait_ge(x_add, n)
                if later(g):
                    dve.wait_ge(grp_add, g)
                dve.wait_ge(grp_mm, g + 1)
                there = acc[:, bass.ds(col, WC)]
                dve.tensor_tensor(there, psE[s % 4][:, 0:WC], there, ALU.add).then_inc(grp_add, 1)

            def own(i):
                dve.wait_ge(own_h, i + 1)
                dve.tensor_tensor(xb[:, blk(i)], xb[:, blk(i)], h_own[:, :], ALU.add).then_inc(own_add, 1)
                dve.wait_ge(own_mm, i + 1)
                dve.tensor_tensor(own_sum[:, :], psM[0][:, 0:TD], bn[:, :], ALU.add).then_inc(own_rd, 1)
                dve.wait_ge(own_rd, i + 1)
                for t in range(T):
                    dve.wait_ge(own_add, 4 * i + (t + 1))
                    dve.scalar_tensor_tensor(
                        out=xb[:, blk(i)], in0=own_sum[:, t * D:(t + 1) * D], scalar=mask[:, t, bass.ds(i, 1)],
                        in1=xb[:, blk(i)], op0=ALU.mult, op1=ALU.add).then_inc(own_add, 1)

            def finish(i):
                dve.wait_ge(own_add, 4 * i + 4)
                dve.wait_ge(fin_mm, i + 2)
                for t in range(T):
                    dve.scalar_tensor_tensor(
                        out=xb[:, blk(i)], in0=psM[1][:, t * D:(t + 1) * D], scalar=mask[:, t, bass.ds(i, 1)],
                        in1=xb[:, blk(i)], op0=ALU.mult, op1=ALU.add).then_inc(fin_part if t < T - 1 else fin_ok, 1)
                    if t < T - 1:
                        dve.wait_ge(fin_part, (T - 1) * i + (t + 1))

            def finish_to(end, always):
                if always:
                    with dve.Fori(dve.snap(done, min_val=0, max_val=NB - 1), end) as i:
                        finish(i)
                    return
                with dve.If(end > dve.snap(done, min_val=0, max_val=NB - 1)):
                    with dve.Fori(dve.snap(done, min_val=0, max_val=NB - 1), end) as i:
                        finish(i)
                    dve.reg_mov(done, end)

            def round_(r):
                for s in range(SLOTS):
                    hot(r * SLOTS + (s + 1), (s + 1) % SLOTS)
                    add(r * SLOTS + s, s)
                    if s == 6 and in_order(r):
                        own(r)
                    if s == 7 and later(r):
                        finish_to(dve.value_load(upto[0:1, bass.ds(r - 1, 1)], min_val=0, max_val=NF), False)
            hot(0, 0)
            round_(0)
            with dve.Fori(1, NB) as r:
                round_(r)
            for r in range(NB, IT):
                round_(r)
            for g in range(IT * SLOTS, G):
                if g + 1 < G:
                    hot(g + 1, (g + 1) % SLOTS)
                add(g, g % SLOTS)
            finish_to(NB, True)


_INS = ["x", "src", "dst", "edge_type_3", "node_type_3", "L0_gnn_W_e", "L0_gnn_b_e", "L0_gnn_W_n", "L0_gnn_b_n"]


def kernel(**inputs):
    import numpy as _np
    import concourse.bacc as _bacc
    from concourse import mybir as _mybir
    from concourse.bass_utils import run_bass_kernel_spmd as _run

    nc = _bacc.Bacc("TRN2", target_bir_lowering=False, num_devices=1)
    arrays, args = {}, []
    for name in _INS:
        a = _np.ascontiguousarray(inputs[name])
        arrays[f"in_{name}_dram"] = a
        args.append(nc.dram_tensor(f"in_{name}_dram", a.shape, _mybir.dt.from_np(a.dtype), kind="ExternalInput").ap())
    shape = _np.shape(inputs["x"])
    out = nc.dram_tensor("out_dram", shape, _mybir.dt.float32, kind="ExternalOutput").ap()
    build(nc, *args, out)
    r = _run(nc, [arrays], core_ids=[0])
    return r.results[0]["out_dram"]
```

```python
import concourse.bass as bass
from concourse import mybir
from contextlib import ExitStack

F32 = mybir.dt.float32
I32 = mybir.dt.int32
BF16 = mybir.dt.bfloat16
ALU = mybir.AluOpType
ACT = mybir.ActivationFunctionType
AX_X = mybir.AxisListType.X

P = 128
T = 3
EPS = 1e-5
TPG = 4
GE = TPG * P
SLOTS = 8
WIN = 32
WC = WIN * T
PAD_TYPE = -100000
UN = 4
CHUNKS = (8, 24)
FAR = 1 << 20


def build(nc, x, src, dst, etype, ntype, w_e, b_e, w_n, b_n, out):
    N, D = x.shape
    E = src.shape[0]
    NB = -(-N // P)
    NF = N // P
    NR = N - NF * P
    G = -(-E // GE)
    GF = E // GE
    ER = E - GF * GE
    GB = -(-G // P)
    TD = T * D
    IT = NB - 1
    GT = IT * SLOTS
    K = G - GT
    AW = max(N + WIN, NB * P) * T
    NP = D // P + T
    MB = 64
    PB = P.bit_length() - 1
    assert 1 < K < IT - 1 and IT < MB and MB * SLOTS == GB * P
    assert GT // P == GB - 1 and GF == G - 1 and K < P
    assert SLOTS >= 2 * TPG and 4 * TPG * WC == T * NP * D
    assert D == P and NR and ER and NB % UN == 1 and GF < GB * P

    table = nc.dram_tensor("message_table", [N, TD], F32, kind="Internal").ap()
    table_rows = table.rearrange("n (t d) -> (n t) d", t=T)

    with ExitStack() as ctx:
        def sb(name, shape, dt=F32):
            return ctx.enter_context(nc.sbuf_tensor(name, shape, dt))

        def sem(name):
            return ctx.enter_context(nc.semaphore(name))

        acc = sb("acc", [P, AW])
        xb = sb("xb", [P, NB * D])
        rows = sb("rows", [P, SLOTS, TPG, D])
        raw = sb("raw", [P, K, TPG, D])
        onehot = sb("onehot", [P, 4, TPG, WC])
        onehot_raw = sb("onehot_raw", [P, TPG, WC])
        onehot_x = sb("onehot_x", [P, TPG, WC])
        iota_w = sb("iota_w", [P, WC])
        iota_p = sb("iota_p", [P, P])
        iota_c = sb("iota_c", [P, 1])
        ident = sb("ident", [P, P])
        EW = GB * GE
        e_src, e_dst, e_typ = (acc[:, k * EW:(k + 1) * EW].rearrange("p (b j) -> p b j", b=GB).bitcast(I32)
                               for k in range(3))
        e_idx, e_key = (acc[:, k * EW:(k + 1) * EW].rearrange("p (b j) -> p b j", b=GB) for k in range(2))
        lo = sb("lo", [P, GB])
        hi = sb("hi", [P, GB])
        lo3 = sb("lo3", [P, GB])
        span = sb("span", [P, GB])
        idx = sb("idx", [P, G, TPG], I32)
        idx_raw = sb("idx_raw", [P, K, TPG], I32)
        key = sb("key", [P, G, TPG])
        idx_now = sb("idx_now", [P, SLOTS, TPG], I32)
        key_x = sb("key_x", [P, 2, TPG])
        ctrl = sb("ctrl", [1, 2, G], I32)
        span_i = acc[0:1, 0:G].bitcast(I32)
        ahead = sb("ahead", [1, 2, 2 * MB])
        ahead_i = sb("ahead_i", [1, 2, MB], I32)
        upto = sb("upto", [1, MB], I32)
        bound = sb("bound", [1, MB])
        spare = rows[:, :, :, :].rearrange("p s u d -> p (s u d)")
        we_raw = spare[:, 0:TD].rearrange("p (t i) -> p t i", t=T)
        be = spare[0:T, TD:2 * TD]
        be_p = spare[0:T, 2 * TD:4 * TD].rearrange("t (k o) -> t k o", k=2)
        raw_f32 = spare[0:K, 6 * TD:6 * TD + GE]
        be_h = spare[0:T, 4 * TD:4 * TD + 3 * TD // 2].bitcast(BF16).rearrange("t (k o) -> t k o", k=3)
        wn_raw = onehot[:, :, :, :].rearrange("p a u w -> p (a u w)").rearrange("p (t i) -> p t i", t=T)
        weT = sb("weT", [P, TD])
        wnT = sb("wnT", [P, NP, TD])
        be_3 = sb("be_3", [T, TD], BF16)
        ones = sb("ones", [T, P], BF16)
        pick = sb("pick", [T, 3])
        bn = sb("bn", [P, TD])
        nt_raw = onehot_x[:, :, :].rearrange("p u w -> p (u w)")[:, 0:P].bitcast(I32)
        nt_f = sb("nt_f", [P, P])
        ntT = sb("ntT", [P, NB])
        mask = sb("mask", [P, T, NB])
        stats = sb("stats", [P, 4, 6])
        mv = sb("mv", [P, NB, 2])
        std = sb("std", [P, NB])
        rstd = sb("rstd", [P, NB])
        nbias = sb("nbias", [P, NB])
        raw_mv = sb("raw_mv", [P, TPG, 2])
        raw_std = sb("raw_std", [P, TPG])
        raw_rstd = sb("raw_rstd", [P, TPG])
        raw_nbias = sb("raw_nbias", [P, TPG])
        eps = sb("eps", [P, 1])
        zero = sb("zero", [P, 1])
        h = sb("h", [P, 4, D])
        hT = sb("hT", [P, 4, P])
        msg = sb("msg", [P, 4, TD])
        h_own = sb("h_own", [P, D])
        hT_own = sb("hT_own", [P, P])
        own_sum = sb("own_sum", [P, TD])
        stage = sb("stage", [P, T, P])

        psT = [ctx.enter_context(nc.psum_tensor(f"psT{i}", [P, 512], F32)) for i in range(2)]
        psM = [ctx.enter_context(nc.psum_tensor(f"psM{i}", [P, 512], F32)) for i in range(2)]
        psE = [ctx.enter_context(nc.psum_tensor(f"psE{i}", [P, 512], F32)) for i in range(4)]
        psH = [psM[0], psM[1], psE[2], psE[3]]

        edges_in = sem("edges_in")
        x_in = [sem(f"x_in{i}") for i in range(3)]
        we_in = sem("we_in")
        wn_in = sem("wn_in")
        be_in = sem("be_in")
        small_in = sem("small_in")
        zeroed = sem("zeroed")
        consts = sem("consts")
        ident_ok = sem("ident_ok")
        types_ok = sem("types_ok")
        bias_ok = sem("bias_ok")
        pads = sem("pads")
        xpad = sem("xpad")
        acc_top = sem("acc_top")
        idx_f = sem("idx_f")
        raw_in = sem("raw_in")
        raw_f = sem("raw_f")
        raw_ft = sem("raw_ft")
        raw_ix = sem("raw_ix")
        dv = sem("dv")
        w_t = sem("w_t")
        w_c = sem("w_c")
        stat = sem("stat")
        var_ok = sem("var_ok")
        std_ok = sem("std_ok")
        norm_ok = sem("norm_ok")
        key_ok = sem("key_ok")
        idx_t = sem("idx_t")
        idx_c = sem("idx_c")
        key_t = sem("key_t")
        key_c = sem("key_c")
        ctl_t = sem("ctl_t")
        ctrl_ok = sem("ctrl_ok")
        h_ok = sem("h_ok")
        h_t = sem("h_t")
        hT_ok = sem("hT_ok")
        tab_mm = sem("tab_mm")
        tab_msg = [sem(f"tab_msg{i}") for i in range(4)]
        tab_out = [sem(f"tab_out{i}") for i in range(4)]
        idx_st = sem("idx_st")
        landed = [sem(f"landed{i}") for i in range(SLOTS)]
        hot_ok = sem("hot_ok")
        grp_mm = sem("grp_mm")
        grp_add = sem("grp_add")
        xkey = sem("xkey")
        xhot_ok = sem("xhot_ok")
        x_mm = sem("x_mm")
        x_add = sem("x_add")
        own_h = sem("own_h")
        own_t = sem("own_t")
        own_st = sem("own_st")
        own_mm = sem("own_mm")
        own_rd = sem("own_rd")
        own_add = sem("own_add")
        raw_landed = sem("raw_landed")
        raw_stat = sem("raw_stat")
        raw_var = sem("raw_var")
        raw_dev = sem("raw_dev")
        raw_inv = sem("raw_inv")
        raw_norm = sem("raw_norm")
        raw_h = sem("raw_h")
        raw_t = sem("raw_t")
        raw_hT = sem("raw_hT")
        raw_mm = sem("raw_mm")
        raw_msg = sem("raw_msg")
        raw_hot = sem("raw_hot")
        raw_sum = sem("raw_sum")
        raw_add = sem("raw_add")
        fin_st = sem("fin_st")
        fin_mm = sem("fin_mm")
        fin_part = sem("fin_part")
        fin_ok = sem("fin_ok")
        fin_out = sem("fin_out")

        assert TPG * WC >= P and 6 * TD + GE <= SLOTS * TPG * D


        def blk(i):
            return bass.ds(i * D, D)

        def later(i, first=1):
            return not isinstance(i, int) or i >= first

        def steps(eng, first, last, unroll, step):
            loops = (last - first) // unroll
            if loops > 1:
                with eng.Fori(0, loops) as r:
                    for s in range(unroll):
                        step(r * unroll + (first + s), (first + s) % unroll)
                first += loops * unroll
            for i in range(first, last):
                step(i, i % unroll)

        EDGE_LOADS = 3 * (GB + 1) + 1
        CUTS = (0,) + CHUNKS + (NB,)
        block = ctx.enter_context(nc.Block())

        @block.sync
        def _(sp):
            sp.dma_start(e_src[0:K, 0, :], src[0:K * GE].rearrange("(r j) -> r j", j=GE)).then_inc(raw_in, 16)
            for c in range(3):
                a, b = CUTS[c], min(CUTS[c + 1], NF)
                sp.dma_start(xb[:, a * D:b * D],
                             x[a * P:b * P, :].rearrange("(b p) d -> p b d", p=P)).then_inc(x_in[c], 16)
            sp.wait_ge(xpad, 1)
            sp.dma_start(xb[0:NR, NF * D:NB * D], x[NF * P:N, :]).then_inc(x_in[2], 16)
            sp.wait_ge(pads, 3)
            for a, e0 in ((e_src, src), (e_typ, etype), (e_dst, dst)):
                for b in range(GB):
                    m, n = K if b == 0 and e0 is src else 0, min(P, GF - b * P)
                    sp.dma_start(a[m:n, b, :], e0[(b * P + m) * GE:(b * P + n) * GE]
                                 .rearrange("(r j) -> r j", j=GE)).then_inc(edges_in, 16)
                r = GF % P
                sp.dma_start(a[r:r + 1, GB - 1, 0:ER],
                             e0[GF * GE:E].rearrange("(r j) -> r j", r=1)).then_inc(edges_in, 16)
            sp.dma_start(e_dst[r:r + 1, GB - 1, ER:GE],
                         dst[E - (GE - ER):E].rearrange("(r j) -> r j", r=1)).then_inc(edges_in, 16)

            with sp.Fori(0, NF // UN) as r:
                for s in range(UN):
                    sp.wait_ge(tab_msg[s], r + 1)
                    sp.dma_start(table[bass.ds(r * (UN * P) + s * P, P), :], msg[:, s, :]).then_inc(tab_out[s], 16)
            sp.wait_ge(tab_msg[0], NF // UN + 1)
            sp.dma_start(table[NF * P:N, :], msg[0:NR, 0, :]).then_inc(tab_out[0], 16)

            with sp.Fori(0, NF) as i:
                sp.wait_ge(fin_ok, i + 2)
                sp.dma_start(out[bass.ds(i * P, P), :], xb[:, blk(i)]).then_inc(fin_out, 16)
            sp.wait_ge(fin_ok, NB + 1)
            sp.dma_start(out[NF * P:N, :], xb[0:NR, blk(NF)]).then_inc(fin_out, 16)
            sp.wait_ge(fin_out, 16 * NB)

        @block.gpsimd
        def _(pool):
            pool.iota(iota_p[:, :], [[1, P]], base=0, channel_multiplier=0,
                      allow_small_or_imprecise_dtypes=True).then_inc(consts, 1)
            pool.iota(iota_c[:, :], [[0, 1]], base=0, channel_multiplier=1,
                      allow_small_or_imprecise_dtypes=True).then_inc(consts, 1)
            pool.memset(xb[:, NF * D:NB * D], 0.0).then_inc(xpad, 1)
            pool.memset(e_src[:, GB - 1, :], 0).then_inc(pads, 1)
            pool.memset(e_typ[:, GB - 1, :], PAD_TYPE).then_inc(pads, 1)
            pool.memset(e_dst[:, GB - 1, :], FAR).then_inc(pads, 1)
            pool.iota(iota_w[:, :], [[1, WC]], base=0, channel_multiplier=0,
                      allow_small_or_imprecise_dtypes=True).then_inc(consts, 1)
            pool.wait_ge(raw_ix, 1)
            for k in range(K):
                for u in range(TPG):
                    pool.indirect_dma_start(
                        out=raw[:, k, u, :], out_offset=None, in_=x,
                        in_offset=bass.IndirectOffsetOnAxis(ap=idx_raw[:, k, u:u + 1], axis=0),
                    ).then_inc(raw_landed, 16)
            for s in range(UN):
                pool.wait_ge(tab_out[s], 16 * len(range(s, NB, UN)))
            due = pool.alloc_register("due")
            pool.reg_mov(due, 1)

            def gather(g, s):
                if isinstance(g, int):
                    pool.wait_ge(idx_st, g + 1)
                else:
                    pool.wait_ge(idx_st, pool.snap(due, min_val=1))
                    pool.reg_add(due, due, 1)
                for u in range(TPG):
                    pool.indirect_dma_start(
                        out=rows[:, s, u, :], out_offset=None, in_=table_rows,
                        in_offset=bass.IndirectOffsetOnAxis(ap=idx_now[:, s, u:u + 1], axis=0),
                    ).then_inc(landed[s], 16)
            steps(pool, 0, GT, SLOTS, gather)

        @block.tensor
        def _(pe):
            pe.sem_inc(fin_mm, 1)
            n = [0]

            def weight(a):
                if n[0] >= 2:
                    pe.wait_ge(w_c, n[0] - 1)
                pe.transpose(psT[n[0] % 2][:, 0:P], a, ident[:, :]).then_inc(w_t, 1)
                n[0] += 1

            pe.wait_ge(ident_ok, 1)
            pe.wait_ge(raw_f, 1)
            for u in range(TPG):
                m = pe.transpose(psE[0][:, u * K:(u + 1) * K], raw_f32[:, u * P:(u + 1) * P], ident[0:K, 0:K])
            m.then_inc(raw_ft, 1)
            pe.wait_ge(we_in, 16)
            for t in range(T):
                weight(we_raw[:, t, :])
            pe.wait_ge(bias_ok, 1)

            def tr(i, s):
                pe.wait_ge(h_ok, i + 1)
                pe.transpose(psT[s % 2][:, 0:P], h[:, s, :], ident[:, :]).then_inc(h_t, 1)

            def mm(i, s, turn):
                if turn is not None:
                    pe.wait_ge(tab_msg[s], turn)
                pe.matmul(psH[s][:, 0:TD], ones[:, :], be_3[:, :], start=True, stop=False)
                pe.wait_ge(hT_ok, i + 1)
                pe.matmul(psH[s][:, 0:TD], hT[:, s, :], weT[:, :], start=False, stop=True).then_inc(tab_mm, 1)

            pe.wait_ge(w_c, n[0])
            tr(0, 0)
            for i in range(UN):
                tr(i + 1, (i + 1) % UN)
                mm(i, i, None)
            with pe.Fori(1, NF // UN) as r:
                for s in range(UN):
                    tr(r * UN + (s + 1), (s + 1) % UN)
                    mm(r * UN + s, s, r)
            mm(NF, 0, NF // UN)

            pe.wait_ge(idx_f, 1)
            for b in range(GB):
                if b >= 2:
                    pe.wait_ge(idx_c, b - 1)
                elif b == 0:
                    pe.wait_ge(raw_ix, 1)
                for u in range(TPG):
                    m = pe.transpose(psE[b % 2][:, u * P:(u + 1) * P], e_idx[:, b, u * P:(u + 1) * P], ident[:, :])
                m.then_inc(idx_t, 1)
            pe.wait_ge(key_ok, 1)
            for b in range(GB):
                if b >= 2:
                    pe.wait_ge(key_c, b - 1)
                else:
                    pe.wait_ge(idx_c, GB - 1 + b)
                for u in range(TPG):
                    m = pe.transpose(psE[b % 2][:, u * P:(u + 1) * P], e_key[:, b, u * P:(u + 1) * P], ident[:, :])
                m.then_inc(key_t, 1)
            for s in (2, 3):
                pe.wait_ge(tab_msg[s], NF // UN)
            for a, q in ((lo, 2), (span, 3)):
                for b in range(GB):
                    m = pe.matmul(psE[q][0:1, b * P:(b + 1) * P], a[:, b:b + 1], ident[:, :], start=True, stop=True)
                m.then_inc(ctl_t, 1)

            pe.wait_ge(wn_in, 16)
            for t in range(T):
                for p in range(NP):
                    weight(wn_raw[:, t, p * D:(p + 1) * D])
            pe.wait_ge(types_ok, 1)
            weight(nt_f[:, :])

            pe.wait_ge(key_c, GB)
            pe.wait_ge(ctrl_ok, 1)
            pe.wait_ge(w_c, n[0])
            for s in (0, 1):
                pe.wait_ge(tab_msg[s], NF // UN)
            pe.wait_ge(tab_msg[0], NF // UN + 1)
            passes = pe.alloc_register("passes")
            pe.reg_mov(passes, 0)
            done = pe.alloc_register("done")
            pe.reg_mov(done, 0)

            def products(bank, hot, parts):
                for cols, tile in parts:
                    for u in range(TPG):
                        m = pe.matmul(bank[:, cols], tile(u), hot[:, u, cols], start=(u == 0), stop=(u == TPG - 1))
                return m

            def passes_past_first(g):
                return pe.value_load(ctrl[0:1, 1, bass.ds(g, 1)], min_val=0, max_val=N // WIN)

            def further_passes(more, parts):
                with pe.If(more > 0):
                    with pe.Fori(0, more) as _k:
                        pe.reg_add(passes, passes, 1)
                        pe.wait_ge(xhot_ok, pe.snap(passes, min_val=1))
                        products(psT[0], onehot_x, parts).then_inc(x_mm, 1)

            def group(g, s):
                parts = [(slice(0, WC), lambda u: rows[:, s, u, :])]
                more = passes_past_first(K + g)
                turn = g // SLOTS + 1 if isinstance(g, int) else None
                pe.wait_ge(landed[s], 16 * TPG * turn if turn else (g - s) * (16 * TPG // SLOTS) + 16 * TPG)
                further_passes(more, parts)
                pe.wait_ge(hot_ok, g + 1)
                if later(g, 2):
                    pe.wait_ge(grp_add, g - 1)
                products(psE[s % 2], onehot[:, s % 4, :, :], parts).then_inc(grp_mm, 1)

            def raw_transpose(r):
                pe.wait_ge(raw_h, r * TPG + TPG)
                for u in range(TPG):
                    m = pe.transpose(psE[2][:, u * P:(u + 1) * P], h[:, u, :], ident[:, :])
                m.then_inc(raw_t, 1)

            def raw_multiply(r, u):
                if u == 0:
                    pe.wait_ge(raw_hT, r + 1)
                    if later(r):
                        pe.wait_ge(raw_add, r)
                if u >= 2:
                    pe.wait_ge(raw_msg, r * TPG + (u - 1))
                pe.matmul(psE[3 - u % 2][:, 0:TD], ones[:, :], be_3[:, :], start=True, stop=False)
                pe.matmul(psE[3 - u % 2][:, 0:TD], hT[:, u, :], weT[:, :], start=False, stop=True).then_inc(raw_mm, 1)

            def raw_group(r):
                parts = [(slice(t, WC, T), lambda u, t=t: msg[:, u, t * D:(t + 1) * D]) for t in range(T)]
                more = passes_past_first(r)
                pe.wait_ge(raw_msg, r * TPG + TPG)
                further_passes(more, parts)
                pe.wait_ge(raw_hot, r + 1)
                products(psE[3], onehot_raw, parts).then_inc(raw_sum, 1)

            def own_tr(i):
                pe.wait_ge(own_h, i + 1)
                pe.transpose(psT[1][:, 0:P], h_own[:, :], ident[:, :]).then_inc(own_t, 1)

            def own_mul(i):
                pe.wait_ge(own_st, i + 1)
                if later(i):
                    pe.wait_ge(own_rd, i)
                pe.matmul(psM[0][:, 0:TD], hT_own[:, :], wnT[:, 0, :], start=True, stop=True).then_inc(own_mm, 1)

            def finish(i):
                pe.wait_ge(fin_st, i + 1)
                pe.wait_ge(fin_ok, i + 1)
                for t in range(T):
                    m = pe.matmul(psM[1][:, 0:TD], stage[:, t, :], wnT[:, 1 + t, :], start=(t == 0), stop=(t == T - 1))
                m.then_inc(fin_mm, 1)

            def finish_to(end, always):
                if always:
                    with pe.Fori(pe.snap(done, min_val=0, max_val=NB - 1), end) as i:
                        finish(i)
                    return
                with pe.If(end > pe.snap(done, min_val=0, max_val=NB - 1)):
                    with pe.Fori(pe.snap(done, min_val=0, max_val=NB - 1), end) as i:
                        finish(i)
                    pe.reg_mov(done, end)

            def round_(r, with_raw):
                last = isinstance(r, int) and r == IT - 1
                for s in range(SLOTS):
                    group(r * SLOTS + s, s)
                    if s == 2:
                        own_tr(r + 1)
                    if s == 3 and with_raw:
                        raw_transpose(r)
                    if s in (5, 6) and with_raw:
                        raw_multiply(r, (s - 5) * 2)
                        raw_multiply(r, (s - 5) * 2 + 1)
                    if s == 5:
                        own_mul(r + 1)
                    if s == 7 and with_raw:
                        raw_group(r)
                    if last and s == 4:
                        finish_to(pe.value_load(upto[0:1, IT - 1:IT], min_val=0, max_val=NF), False)
                    if s == (1 if last else 7) and later(r):
                        finish_to(pe.value_load(upto[0:1, bass.ds(r - 1, 1)], min_val=0, max_val=NF), False)
            own_tr(0)
            own_mul(0)
            round_(0, True)
            with pe.Fori(1, K) as r:
                round_(r, True)
            with pe.Fori(K, IT - 1) as r:
                round_(r, False)
            round_(IT - 1, False)
            finish_to(NB, True)

        @block.scalar
        def _(act):
            act.dma_start(be, b_e.rearrange("(a t) o -> a (t o)", a=1).to_broadcast([T, TD])).then_inc(be_in, 16)
            act.dma_start(we_raw[:, :, :], w_e.rearrange("t o i -> o t i")).then_inc(we_in, 16)
            act.dma_start(wn_raw[:, :, :], w_n.rearrange("t o i -> o t i")).then_inc(wn_in, 16)
            act.wait_ge(zeroed, 1)
            act.dma_start(nt_raw[0:NF, :], ntype[0:NF * P].rearrange("(b p) -> b p", p=P)).then_inc(small_in, 16)
            act.dma_start(nt_raw[NF:NB, 0:NR], ntype[NF * P:N].rearrange("(b p) -> b p", b=1)).then_inc(small_in, 16)
            act.dma_start(bn[:, :], b_n.rearrange("(a t) o -> a (t o)", a=1).to_broadcast([P, TD])).then_inc(small_in, 16)
            n = [0]

            def weight(o, a):
                act.wait_ge(w_t, n[0] + 1)
                act.copy(o, psT[n[0] % 2][:, 0:a]).then_inc(w_c, 1)
                n[0] += 1

            def deviations(c):
                a, b = CUTS[c], CUTS[c + 1]
                act.wait_ge(var_ok, c + 1)
                act.activation(std[:, a:b], mv[:, a:b, 1], ACT.Sqrt, bias=eps[:, 0:1]).then_inc(std_ok, 1)

            def norm_into(o, i):
                return act.activation(o, xb[:, blk(i)], ACT.Relu, scale=rstd[:, bass.ds(i, 1)],
                                      bias=nbias[:, bass.ds(i, 1)])

            def norm(i, s):
                norm_into(h[:, s, :], i).then_inc(h_ok, 1)

            def copy_t(i, s):
                act.wait_ge(h_t, i + 1)
                if later(i, 4):
                    act.wait_ge(tab_mm, i - 3)
                act.copy(hT[:, s, :], psT[s % 2][:, 0:P]).then_inc(hT_ok, 1)

            def relu(i, s):
                act.wait_ge(tab_mm, i + 1)
                if later(i, UN):
                    act.wait_ge(tab_out[s], (i - s) * (16 // UN))
                act.activation(msg[:, s, :], psH[s][:, 0:TD], ACT.Relu).then_inc(tab_msg[s], 1)

            def step(i, s):
                if not isinstance(i, int) or i + 1 < NB:
                    norm(i + 1, (s + 1) % UN)
                copy_t(i, s)
                if s % 2 == 1:
                    relu(i - 1, s - 1)
            act.wait_ge(zeroed, 2)
            quarter = -(-(AW - 3 * EW) // 4)

            def zero_acc(q):
                a, b = 3 * EW + q * quarter, min(3 * EW + (q + 1) * quarter, AW)
                act.copy(acc[:, a:b], zero[:, 0:1].to_broadcast([P, b - a])).then_inc(acc_top, 1)
            zero_acc(0)
            zero_acc(1)
            deviations(0)
            for t in range(T):
                weight(weT[:, t * D:(t + 1) * D], P)
            act.wait_ge(norm_ok, 1)
            norm(0, 0)
            a = CHUNKS[0] - 1
            for i in range(a):
                step(i, i % UN)
            deviations(1)
            act.wait_ge(norm_ok, 2)
            b = CHUNKS[1] - 1
            steps(act, a, b, UN, step)
            deviations(2)
            act.wait_ge(norm_ok, 3)
            steps(act, b, NB - 1, UN, step)
            step(NB - 1, (NB - 1) % UN)
            relu(NB - 1, (NB - 1) % UN)

            for b in range(GB):
                k = min(P, G - b * P)
                act.wait_ge(idx_t, b + 1)
                act.copy(idx[:, b * P:b * P + k, :].rearrange("p g u -> p u g"),
                         psE[b % 2][:, :].rearrange("p (u g) -> p u g", u=TPG)[:, :, 0:k]).then_inc(idx_c, 1)

            def stage_idx(g, s):
                if later(g, SLOTS):
                    act.wait_ge(grp_mm, g - (SLOTS - 1))
                act.copy(idx_now[:, s, :],
                         idx[:, bass.ds(K + g, 1), :].rearrange("p g u -> p (g u)")).then_inc(idx_st, 1)
            act.wait_ge(idx_c, GB)
            for g in range(SLOTS):
                stage_idx(g, g)
            zero_acc(2)
            zero_acc(3)
            for t in range(T):
                for p in range(NP):
                    weight(wnT[:, p, t * D:(t + 1) * D], P)
            weight(ntT[:, :], NB)

            done = act.alloc_register("done")
            act.reg_mov(done, 0)

            def own_norm(i):
                if later(i):
                    act.wait_ge(own_add, 4 * i - 3)
                norm_into(h_own[:, :], i).then_inc(own_h, 1)

            def own_copy(i):
                act.wait_ge(own_t, i + 1)
                if later(i):
                    act.wait_ge(own_mm, i)
                act.copy(hT_own[:, :], psT[1][:, 0:P]).then_inc(own_st, 1)

            def finish(i):
                act.wait_ge(fin_mm, i + 1)
                act.copy(stage[:, :, :],
                         acc[:, bass.ds(i * (P * T), P * T)].rearrange("p (n t) -> p t n", t=T)).then_inc(fin_st, 1)

            def finish_to(end, always):
                if always:
                    with act.Fori(act.snap(done, min_val=0, max_val=NB - 1), end) as i:
                        finish(i)
                    return
                with act.If(end > act.snap(done, min_val=0, max_val=NB - 1)):
                    with act.Fori(act.snap(done, min_val=0, max_val=NB - 1), end) as i:
                        finish(i)
                    act.reg_mov(done, end)

            def raw_deviations(r):
                act.wait_ge(raw_var, r * TPG + TPG)
                act.activation(raw_std[:, :], raw_mv[:, :, 1], ACT.Sqrt, bias=eps[:, 0:1]).then_inc(raw_dev, 1)

            def raw_normalise(r):
                act.wait_ge(raw_norm, r + 1)
                for u in range(TPG):
                    act.activation(h[:, u, :], raw[:, bass.ds(r, 1), u, :].rearrange("p k d -> p (k d)"), ACT.Relu,
                                   scale=raw_rstd[:, u:u + 1], bias=raw_nbias[:, u:u + 1]).then_inc(raw_h, 1)

            def raw_copy(r):
                act.wait_ge(raw_t, r + 1)
                act.copy(hT[:, :, :], psE[2][:, :].rearrange("p (u e) -> p u e", u=TPG)).then_inc(raw_hT, 1)

            def raw_relu(r, u):
                act.wait_ge(raw_mm, r * TPG + (u + 1))
                if u == 0 and later(r):
                    act.wait_ge(raw_sum, r)
                act.activation(msg[:, u, :], psE[3 - u % 2][:, 0:TD], ACT.Relu).then_inc(raw_msg, 1)

            def round_(r, with_raw):
                last = isinstance(r, int) and r == IT - 1
                for s in range(SLOTS):
                    if not last:
                        stage_idx((r + 1) * SLOTS + s, s)
                    if s == 0:
                        own_norm(r + 1)
                        if with_raw:
                            raw_deviations(r)
                    if s == 1 and with_raw:
                        raw_normalise(r)
                    if s == 3:
                        if with_raw:
                            raw_copy(r)
                        own_copy(r + 1)
                    if s in (4, 5) and with_raw:
                        raw_relu(r, (s - 4) * 2)
                        raw_relu(r, (s - 4) * 2 + 1)
                    if last and s == 4:
                        act.wait_ge(grp_add, GT - SLOTS // 2)
                        finish_to(act.value_load(upto[0:1, IT - 1:IT], min_val=0, max_val=NF), False)
                    if s == (1 if last else 5) and later(r):
                        act.wait_ge(grp_add, r * SLOTS)
                        if with_raw:
                            act.wait_ge(raw_add, r)
                        finish_to(act.value_load(upto[0:1, bass.ds(r - 1, 1)], min_val=0, max_val=NF), False)
            act.wait_ge(ctrl_ok, 1)
            own_norm(0)
            own_copy(0)
            for s in range(UN):
                act.wait_ge(tab_out[s], 16 * len(range(s, NB, UN)))
            round_(0, True)
            with act.Fori(1, K) as r:
                round_(r, True)
            act.wait_ge(raw_add, K)
            with act.Fori(K, IT - 1) as r:
                round_(r, False)
            round_(IT - 1, False)
            act.wait_ge(grp_add, GT)
            finish_to(NB, True)

        @block.vector
        def _(dve):
            c = [0]

            def link(ins):
                c[0] += 1
                ins.then_inc(dv, 1)
                dve.wait_ge(dv, c[0])

            dve.sem_inc(fin_ok, 1)
            dve.memset(nt_raw[:, :], 0).then_inc(zeroed, 1)
            dve.memset(eps[:, :], EPS)
            dve.memset(zero[:, :], 0.0).then_inc(zeroed, 1)
            dve.memset(ones[:, :], 1.0)
            for k in range(2):
                link(dve.memset(ahead[:, k, :], float(FAR)))
            dve.wait_ge(consts, 2)
            dve.tensor_scalar(ident[:, :], iota_p[:, :], iota_c[:, 0:1], None, ALU.is_equal).then_inc(ident_ok, 1)
            dve.wait_ge(raw_in, 16)
            dve.tensor_copy(raw_f32, e_src[0:K, 0, :]).then_inc(raw_f, 1)
            dve.wait_ge(raw_ft, 1)
            dve.tensor_copy(idx_raw[:, :, :].rearrange("p k u -> p u k"),
                            psE[0][:, 0:TPG * K].rearrange("p (u k) -> p u k", u=TPG)).then_inc(raw_ix, 1)
            for k in range(3):
                link(dve.tensor_scalar(pick[:, k:k + 1], iota_c[0:T, 0:1], float(k), None, ALU.is_equal))
            link(dve.tensor_scalar(bound[:, :], iota_p[0:1, 0:MB], 2.0, float(2 * K - 5), ALU.mult, ALU.subtract))
            link(dve.tensor_scalar(bound[:, :], bound[:, :], 2.0, None, ALU.max))
            link(dve.tensor_tensor(bound[:, :], bound[:, :], iota_p[0:1, 1:MB + 1], ALU.min))
            dve.wait_ge(be_in, 16)
            link(dve.tensor_copy(be_h[:, 0, :], be))
            link(dve.tensor_tensor(be_p[:, 0, :], be, be_h[:, 0, :], ALU.subtract))
            link(dve.tensor_copy(be_h[:, 1, :], be_p[:, 0, :]))
            link(dve.tensor_tensor(be_p[:, 1, :], be_p[:, 0, :], be_h[:, 1, :], ALU.subtract))
            link(dve.tensor_copy(be_h[:, 2, :], be_p[:, 1, :]))
            link(dve.tensor_scalar(be_3[:, :], be_h[:, 0, :], pick[:, 0:1], None, ALU.mult))
            link(dve.scalar_tensor_tensor(out=be_3[:, :], in0=be_h[:, 1, :], scalar=pick[:, 1:2], in1=be_3[:, :],
                                          op0=ALU.mult, op1=ALU.add))
            dve.scalar_tensor_tensor(out=be_3[:, :], in0=be_h[:, 2, :], scalar=pick[:, 2:3], in1=be_3[:, :],
                                     op0=ALU.mult, op1=ALU.add).then_inc(bias_ok, 1)

            def sums(i):
                dve.bn_stats(stats[:, i % 4, :], xb[:, i * D:(i + 1) * D]).then_inc(stat, 1)

            def moments(i):
                dve.wait_ge(stat, i + 1)
                return dve.bn_aggr(mv[:, i, :], stats[:, i % 4, :])

            def chunk_stats(a, b):
                sums(a)
                for i in range(a, b):
                    if i + 1 < b:
                        sums(i + 1)
                    m = moments(i)
                m.then_inc(var_ok, 1)

            def inverses(k):
                a, b = CUTS[k], CUTS[k + 1]
                dve.wait_ge(std_ok, k + 1)
                link(dve.reciprocal(rstd[:, a:b], std[:, a:b]))
                dve.scalar_tensor_tensor(out=nbias[:, a:b], in0=mv[:, a:b, 0], scalar=-1.0, in1=rstd[:, a:b],
                                         op0=ALU.mult, op1=ALU.mult).then_inc(norm_ok, 1)

            def relu(i, s):
                dve.wait_ge(tab_mm, i + 1)
                if later(i, UN):
                    dve.wait_ge(tab_out[s], (i - s) * (16 // UN))
                dve.tensor_scalar(msg[:, s, :], psH[s][:, 0:TD], 0.0, None, ALU.max).then_inc(tab_msg[s], 1)

            for k in range(2):
                dve.wait_ge(x_in[k], 16)
                chunk_stats(CUTS[k], CUTS[k + 1])
                inverses(k)
            dve.wait_ge(x_in[2], 32)
            i, last = CUTS[2], CUTS[3]
            sums(i)
            for j in range(1, CHUNKS[1] - 4, 2):
                relu(j, j % UN)
                for _ in range(3):
                    if i < last:
                        if i + 1 < last:
                            sums(i + 1)
                        m = moments(i)
                        i += 1
                        if i == last:
                            m.then_inc(var_ok, 1)
            inverses(2)
            dve.wait_ge(edges_in, 16 * EDGE_LOADS)
            link(dve.scalar_tensor_tensor(out=e_idx, in0=e_src, scalar=float(T), in1=e_typ, op0=ALU.mult, op1=ALU.add))
            dve.tensor_scalar(e_idx[:, GB - 1, :], e_idx[:, GB - 1, :], 0.0, None, ALU.max).then_inc(idx_f, 1)
            j0 = CHUNKS[1] - 4 + 1
            with dve.Fori(0, (NF - j0 + 1) // UN) as r:
                for s in (1, 3):
                    relu(r * UN + (j0 + s - 1), s)

            dve.tensor_reduce(lo[:, :], e_dst, AX_X, ALU.min)
            link(dve.tensor_reduce(hi[:, :], e_dst, AX_X, ALU.max))
            dve.tensor_scalar(lo3[:, :], lo[:, :], float(T), None, ALU.mult)
            dve.tensor_tensor(span[:, :], hi[:, :], lo[:, :], ALU.subtract)
            link(dve.scalar_tensor_tensor(out=e_key, in0=e_dst, scalar=float(T), in1=e_typ, op0=ALU.mult, op1=ALU.add))
            for b in range(GB):
                m = dve.tensor_scalar(e_key[:, b, :], e_key[:, b, :], lo3[:, b:b + 1], None, ALU.subtract)
            m.then_inc(key_ok, 1)
            dve.wait_ge(small_in, 48)
            dve.tensor_copy(nt_f[:, :], nt_raw[:, :]).then_inc(types_ok, 1)
            for b in range(GB):
                dve.wait_ge(key_t, b + 1)
                n = min(P, G - b * P)
                dve.tensor_copy(key[:, b * P:b * P + n, :].rearrange("p g u -> p u g"),
                                psE[b % 2][:, :].rearrange("p (u g) -> p u g", u=TPG)[:, :, 0:n]).then_inc(key_c, 1)

            dve.wait_ge(ctl_t, 2)
            dve.tensor_scalar(ctrl[0:1, 0, :], psE[2][0:1, 0:G], float(T), None, ALU.mult)
            link(dve.tensor_reduce(ahead[:, 0, 0:IT], psE[2][0:1, K:G].rearrange("p (r s) -> p r s", s=SLOTS),
                                   AX_X, ALU.min))
            dve.tensor_tensor(ahead[:, 0, 0:K], ahead[:, 0, 0:K], psE[2][0:1, 0:K], ALU.min)
            dve.tensor_reduce(ahead[:, 0, IT:IT + 1], psE[2][0:1, G - SLOTS // 2:G], AX_X, ALU.min)
            link(dve.tensor_copy(span_i[:, :], psE[3][0:1, 0:G]))
            dve.tensor_scalar(ctrl[0:1, 1, :], span_i[:, :], WIN.bit_length() - 1, None, ALU.arith_shift_right)
            q, d = 0, 1
            while d < MB:
                link(dve.tensor_tensor(ahead[:, 1 - q, 0:MB], ahead[:, q, 0:MB], ahead[:, q, d:MB + d], ALU.min))
                q, d = 1 - q, 2 * d
            link(dve.tensor_copy(ahead_i[:, 0, :], ahead[:, q, 1:MB + 1]))
            link(dve.tensor_scalar(ahead_i[:, 1, :], ahead_i[:, 0, :], PB, None, ALU.arith_shift_right))
            dve.tensor_tensor(upto[:, :], ahead_i[:, 1, :], bound[:, :], ALU.min).then_inc(ctrl_ok, 1)

            link(dve.memset(acc[:, 0:3 * EW], 0.0))
            dve.wait_ge(w_c, T + T * NP + 1)
            for t in range(T):
                m = dve.tensor_scalar(mask[:, t, :], ntT[:, :], float(t), None, ALU.is_equal)
            link(m)

            dve.wait_ge(consts, 3)
            dve.wait_ge(acc_top, 4)
            dve.wait_ge(key_c, GB)
            dve.wait_ge(ctrl_ok, 1)
            passes = dve.alloc_register("passes")
            at = dve.alloc_register("at")
            done = dve.alloc_register("done")
            dve.reg_mov(passes, 0)
            dve.reg_mov(done, 0)
            hot_shape = [P, TPG, WC]
            iota_b = iota_w[:, :].unsqueeze(1).to_broadcast(hot_shape)

            def keys_of(g):
                return key[:, bass.ds(g, 1), :].rearrange("p g u -> p (g u)")

            def hot(g, s):
                if later(g, 4):
                    dve.wait_ge(grp_mm, g - 3)
                dve.tensor_tensor(onehot[:, s % 4, :, :], iota_b, keys_of(K + g).unsqueeze(2).to_broadcast(hot_shape),
                                  ALU.is_equal).then_inc(hot_ok, 1)

            def add_sums(g, last_add, bank, made, count):
                more = dve.value_load(ctrl[0:1, 1, bass.ds(g, 1)], min_val=0, max_val=N // WIN)
                col = dve.value_load(ctrl[0:1, 0, bass.ds(g, 1)], min_val=0, max_val=(N - 1) * T)
                with dve.If(more > 0):
                    dve.tensor_copy(key_x[:, 0, :], keys_of(g))
                    dve.reg_mov(at, col)
                    with dve.Fori(0, more) as _k:
                        last_add()
                        dve.reg_add(passes, passes, 1)
                        n = dve.snap(passes, min_val=1)
                        dve.drain()
                        dve.tensor_scalar(key_x[:, 1, :], key_x[:, 0, :], float(WC), None, ALU.subtract).then_inc(xkey, 1)
                        dve.wait_ge(xkey, n)
                        dve.tensor_copy(key_x[:, 0, :], key_x[:, 1, :])
                        dve.tensor_tensor(onehot_x[:, :, :], iota_b, key_x[:, 1, :].unsqueeze(2).to_broadcast(hot_shape),
                                          ALU.is_equal).then_inc(xhot_ok, 1)
                        dve.wait_ge(x_mm, n)
                        dve.reg_add(at, at, WC)
                        there = acc[:, bass.ds(dve.snap(at, min_val=0, max_val=AW - WC), WC)]
                        dve.tensor_tensor(there, psT[0][:, 0:WC], there, ALU.add).then_inc(x_add, 1)
                        dve.wait_ge(x_add, n)
                last_add()
                dve.wait_ge(made, count)
                there = acc[:, bass.ds(col, WC)]
                return dve.tensor_tensor(there, bank[:, 0:WC], there, ALU.add)

            def add(g, s, raw_before):
                def last_add():
                    if later(g):
                        dve.wait_ge(grp_add, g)
                    if raw_before is not None:
                        dve.wait_ge(raw_add, raw_before)
                add_sums(K + g, last_add, psE[s % 2], grp_mm, g + 1).then_inc(grp_add, 1)

            def raw_moments(r):
                for u in range(TPG):
                    dve.bn_stats(stats[:, u, :],
                                 raw[:, bass.ds(r, 1), u, :].rearrange("p k d -> p (k d)")).then_inc(raw_stat, 1)
                dve.wait_ge(raw_stat, r * TPG + TPG)
                dve.tensor_tensor(onehot_raw[:, :, :], iota_b, keys_of(r).unsqueeze(2).to_broadcast(hot_shape),
                                  ALU.is_equal).then_inc(raw_hot, 1)
                for u in range(TPG):
                    dve.bn_aggr(raw_mv[:, u, :], stats[:, u, :]).then_inc(raw_var, 1)

            def raw_inverses(r):
                dve.wait_ge(raw_dev, r + 1)
                dve.reciprocal(raw_rstd[:, :], raw_std[:, :]).then_inc(raw_inv, 1)
                dve.wait_ge(raw_inv, r + 1)
                dve.scalar_tensor_tensor(out=raw_nbias[:, :], in0=raw_mv[:, :, 0], scalar=-1.0, in1=raw_rstd[:, :],
                                         op0=ALU.mult, op1=ALU.mult).then_inc(raw_norm, 1)

            def raw_add_sums(r):
                add_sums(r, lambda: dve.wait_ge(grp_add, (r + 1) * SLOTS), psE[3], raw_sum, r + 1).then_inc(raw_add, 1)

            def own(i):
                dve.wait_ge(own_h, i + 1)
                dve.tensor_tensor(xb[:, blk(i)], xb[:, blk(i)], h_own[:, :], ALU.add).then_inc(own_add, 1)
                dve.wait_ge(own_mm, i + 1)
                dve.tensor_tensor(own_sum[:, :], psM[0][:, 0:TD], bn[:, :], ALU.add).then_inc(own_rd, 1)
                dve.wait_ge(own_rd, i + 1)
                for t in range(T):
                    dve.wait_ge(own_add, 4 * i + (t + 1))
                    dve.scalar_tensor_tensor(
                        out=xb[:, blk(i)], in0=own_sum[:, t * D:(t + 1) * D], scalar=mask[:, t, bass.ds(i, 1)],
                        in1=xb[:, blk(i)], op0=ALU.mult, op1=ALU.add).then_inc(own_add, 1)

            def finish(i):
                dve.wait_ge(own_add, 4 * i + 4)
                dve.wait_ge(fin_mm, i + 2)
                for t in range(T):
                    dve.scalar_tensor_tensor(
                        out=xb[:, blk(i)], in0=psM[1][:, t * D:(t + 1) * D], scalar=mask[:, t, bass.ds(i, 1)],
                        in1=xb[:, blk(i)], op0=ALU.mult, op1=ALU.add).then_inc(fin_part if t < T - 1 else fin_ok, 1)
                    if t < T - 1:
                        dve.wait_ge(fin_part, (T - 1) * i + (t + 1))

            def finish_to(end, always):
                if always:
                    with dve.Fori(dve.snap(done, min_val=0, max_val=NB - 1), end) as i:
                        finish(i)
                    return
                with dve.If(end > dve.snap(done, min_val=0, max_val=NB - 1)):
                    with dve.Fori(dve.snap(done, min_val=0, max_val=NB - 1), end) as i:
                        finish(i)
                    dve.reg_mov(done, end)

            def round_(r, with_raw):
                last = isinstance(r, int) and r == IT - 1
                for s in range(SLOTS):
                    if not last or s < SLOTS - 1:
                        hot(r * SLOTS + (s + 1), (s + 1) % SLOTS)
                    add(r * SLOTS + s, s, r if s == 0 and with_raw and later(r) else None)
                    if s == 0 and with_raw:
                        raw_moments(r)
                    if s == 1 and with_raw:
                        raw_inverses(r)
                    if s == 6:
                        own(r + 1)
                    if s == 7 and with_raw:
                        raw_add_sums(r)
                    if last and s == 4:
                        finish_to(dve.value_load(upto[0:1, IT - 1:IT], min_val=0, max_val=NF), False)
                    if s == (1 if last else 7) and later(r):
                        finish_to(dve.value_load(upto[0:1, bass.ds(r - 1, 1)], min_val=0, max_val=NF), False)
            hot(0, 0)
            own(0)
            dve.wait_ge(raw_landed, 16 * TPG * K)
            round_(0, True)
            with dve.Fori(1, K) as r:
                round_(r, True)
            dve.wait_ge(raw_add, K)
            with dve.Fori(K, IT - 1) as r:
                round_(r, False)
            round_(IT - 1, False)
            finish_to(NB, True)


_INS = ["x", "src", "dst", "edge_type_3", "node_type_3", "L0_gnn_W_e", "L0_gnn_b_e", "L0_gnn_W_n", "L0_gnn_b_n"]


def kernel(**inputs):
    import numpy as _np
    import concourse.bacc as _bacc
    from concourse import mybir as _mybir
    from concourse.bass_utils import run_bass_kernel_spmd as _run

    nc = _bacc.Bacc("TRN2", target_bir_lowering=False, num_devices=1)
    arrays, args = {}, []
    for name in _INS:
        a = _np.ascontiguousarray(inputs[name])
        arrays[f"in_{name}_dram"] = a
        args.append(nc.dram_tensor(f"in_{name}_dram", a.shape, _mybir.dt.from_np(a.dtype), kind="ExternalInput").ap())
    shape = _np.shape(inputs["x"])
    out = nc.dram_tensor("out_dram", shape, _mybir.dt.float32, kind="ExternalOutput").ap()
    build(nc, *args, out)
    r = _run(nc, [arrays], core_ids=[0])
    return r.results[0]["out_dram"]
```
